# Optimizing a Trainium2 kernel written in Bass

```python
import numpy as np
import jax
import jax.numpy as jnp

def _softmax(x, axis=-1):
    return jax.nn.softmax(x, axis=axis)

def _gelu(x):
    return jax.nn.gelu(x, approximate=True)

def _silu(x):
    return jax.nn.silu(x)

def _sigmoid(x):
    return jax.nn.sigmoid(x)

def _layernorm(x, axis=-1, eps=1e-05):
    m = jnp.mean(x, axis=axis, keepdims=True)
    v = jnp.var(x, axis=axis, keepdims=True)
    return (x - m) / jnp.sqrt(v + eps)

def _scatter_add(tgt, idx, src, axis=0):
    return tgt.at[idx].add(src)

def _segment_sum(src, seg, n):
    return jax.ops.segment_sum(src, seg, n)
kernel_name = 'mk_gnn_preln_d2_gnn_r8_01103a'

def setup_inputs(seed: int=0):
    np.random.seed(seed)
    _w = jnp.asarray

    def _rec_inputs():
        import jax
        import jax.numpy as jnp
        _gk = jax.random.key(seed)
        x = -0.000202 + 1 * jax.random.normal(jax.random.fold_in(_gk, 1), (6250, 128), jnp.float32)
        src = jax.random.randint(jax.random.fold_in(_gk, 2), (200000,), 0, 6250, jnp.int32)
        dst = jax.random.randint(jax.random.fold_in(_gk, 3), (200000,), 0, 6250, jnp.int32)
        _o = jnp.argsort(dst, stable=True)
        src = src[_o]
        dst = dst[_o]
        edge_attr_128 = 2.93046e-05 + 1.00006 * jax.random.normal(jax.random.fold_in(_gk, 11), (200000, 128), jnp.float32)
        return (x, src, dst, edge_attr_128)
    x, src, dst, edge_attr_128 = _rec_inputs()

    def _L0_gnn_setup():
        import jax, jax.numpy as jnp
        import numpy as np
        N = 6250
        E = 100000
        IN = 128
        H = 4
        F = 32
        NEG_SLOPE = 0.2
        key = jax.random.key(seed)
        k1, k2, k3, k4, k5 = jax.random.split(key, 5)
        x = jax.random.normal(k1, (N, IN), dtype=jnp.float32)
        edge_index = jax.random.randint(k2, (2, E), 0, N, dtype=jnp.int32)
        W = jax.random.normal(k3, (IN, H * F), dtype=jnp.float32) * 0.05
        att_src = jax.random.normal(k4, (H, F), dtype=jnp.float32) * 0.05
        att_dst = jax.random.normal(k5, (H, F), dtype=jnp.float32) * 0.05
        bias = jnp.zeros((H * F,), dtype=jnp.float32)
        return {'x': x, 'edge_index': edge_index, 'W': W, 'att_src': att_src, 'att_dst': att_dst, 'bias': bias}
    _L0_gnn_all = _L0_gnn_setup()
    _L0_gnn_in = {k: v for k, v in _L0_gnn_all.items() if k in ('W', 'att_src', 'att_dst', 'bias')}
    del _L0_gnn_all

    def _L1_gnn_setup():
        import jax, jax.numpy as jnp
        import numpy as np
        N, E = (1250, 80000)
        IN_DIM, EDGE_DIM, OUT_DIM = (128, 128, 128)
        key = jax.random.key(seed)
        ks = jax.random.split(key, 9)
        s = 0.02
        return {'x': jax.random.normal(ks[0], (N, IN_DIM), dtype=jnp.float32), 'edge_index': jax.random.randint(ks[1], (2, E), 0, N, dtype=jnp.int64), 'edge_attr': jax.random.normal(ks[2], (E, EDGE_DIM), dtype=jnp.float32), 'We': jax.random.normal(ks[3], (EDGE_DIM, IN_DIM), dtype=jnp.float32) * s, 'be': jnp.zeros((IN_DIM,), dtype=jnp.float32), 'W1': jax.random.normal(ks[4], (2 * IN_DIM, OUT_DIM), dtype=jnp.float32) * s, 'b1': jnp.zeros((OUT_DIM,), dtype=jnp.float32), 'W2': jax.random.normal(ks[5], (OUT_DIM, OUT_DIM), dtype=jnp.float32) * s, 'b2': jnp.zeros((OUT_DIM,), dtype=jnp.float32)}
    _L1_gnn_all = _L1_gnn_setup()
    _L1_gnn_in = {k: v for k, v in _L1_gnn_all.items() if k in ('We', 'be', 'W1', 'b1', 'W2', 'b2')}
    del _L1_gnn_all
    return {'x': x, 'src': src, 'dst': dst, 'edge_attr_128': edge_attr_128, 'L0_gnn_W': _L0_gnn_in['W'], 'L0_gnn_att_src': _L0_gnn_in['att_src'], 'L0_gnn_att_dst': _L0_gnn_in['att_dst'], 'L0_gnn_bias': _L0_gnn_in['bias'], 'L1_gnn_We': _L1_gnn_in['We'], 'L1_gnn_be': _L1_gnn_in['be'], 'L1_gnn_W1': _L1_gnn_in['W1'], 'L1_gnn_b1': _L1_gnn_in['b1'], 'L1_gnn_W2': _L1_gnn_in['W2'], 'L1_gnn_b2': _L1_gnn_in['b2']}

def reference(x, src, dst, edge_attr_128, L0_gnn_W, L0_gnn_att_src, L0_gnn_att_dst, L0_gnn_bias, L1_gnn_We, L1_gnn_be, L1_gnn_W1, L1_gnn_b1, L1_gnn_W2, L1_gnn_b2):
    import jax
    import jax.numpy as jnp

    def _L0_gnn_ref(x, edge_index, W, att_src, att_dst, bias):
        import jax, jax.numpy as jnp
        import numpy as np
        N = 6250
        E = 100000
        IN = 128
        H = 4
        F = 32
        NEG_SLOPE = 0.2
        n = x.shape[0]
        xp = (x @ W).reshape(n, H, F)
        loop = jnp.arange(n, dtype=edge_index.dtype)
        src = jnp.concatenate([edge_index[0], loop])
        dst = jnp.concatenate([edge_index[1], loop])
        a_s = jnp.einsum('nhf,hf->nh', xp, att_src)
        a_d = jnp.einsum('nhf,hf->nh', xp, att_dst)
        e = jax.nn.leaky_relu(a_s[src] + a_d[dst], NEG_SLOPE)
        m = jax.ops.segment_max(e, dst, num_segments=n)
        e = jnp.exp(e - m[dst])
        denom = jax.ops.segment_sum(e, dst, num_segments=n)
        alpha = e / denom[dst]
        msg = alpha[:, :, None] * xp[src]
        out = jax.ops.segment_sum(msg, dst, num_segments=n)
        out = out.reshape(n, H * F) + bias
        return jax.nn.relu(out)

    def _L1_gnn_ref(x, edge_index, edge_attr, We, be, W1, b1, W2, b2):
        import jax, jax.numpy as jnp
        import numpy as np
        N, E = (1250, 80000)
        IN_DIM, EDGE_DIM, OUT_DIM = (128, 128, 128)
        src, dst = (edge_index[0], edge_index[1])
        num_nodes = x.shape[0]
        edge_emb = edge_attr @ We + be
        edge_agg = jax.ops.segment_sum(edge_emb, dst, num_segments=num_nodes)
        x_comb = jnp.concatenate([x, edge_agg], axis=-1)
        neigh = jax.ops.segment_sum(x_comb[src], dst, num_segments=num_nodes)
        h = x_comb + neigh
        return jax.nn.relu(h @ W1 + b1) @ W2 + b2
    edge_index = jnp.stack([src, dst])
    h = jnp.maximum(_layernorm(x, axis=-1), 0.0)
    x = x + _L0_gnn_ref(h, edge_index, L0_gnn_W, L0_gnn_att_src, L0_gnn_att_dst, L0_gnn_bias)
    h = jnp.maximum(_layernorm(x, axis=-1), 0.0)
    x = x + _L1_gnn_ref(h, edge_index, edge_attr_128, L1_gnn_We, L1_gnn_be, L1_gnn_W1, L1_gnn_b1, L1_gnn_W2, L1_gnn_b2)
    return x

_drawn_inputs = setup_inputs


def setup_inputs(seed=0):
    import zlib

    import numpy as np

    out = dict(_drawn_inputs(seed))
    spreads = {'L0_gnn_bias': (0.0, 0.407),
     'L1_gnn_be': (0.0, 0.1),
     'L1_gnn_b1': (0.0, 2.0),
     'L1_gnn_b2': (0.0, 0.306)}
    factors = {'L0_gnn_att_src': 39.566, 'L0_gnn_att_dst': 64.0}
    for name, (base, spread) in spreads.items():
        noise = np.random.default_rng([zlib.crc32(name.encode()), seed]).standard_normal(out[name].shape)
        drawn = base * np.exp(spread * noise) if base else spread * noise
        out[name] = jnp.asarray(drawn.astype(out[name].dtype))
    for name, factor in factors.items():
        out[name] = (out[name] * factor).astype(out[name].dtype)
    return out
```

```python
import concourse.bass as bass
from concourse import mybir
from contextlib import ExitStack

FP32 = mybir.dt.float32
INT32 = mybir.dt.int32
ALU = mybir.AluOpType
ACT = mybir.ActivationFunctionType

N = 6250
E = 200000
C = 128
H = 4
F = C // H
SLOPE = 0.2
EPS = 1e-5

NP = 125
NT = N // NP
SPLIT = 112

J = 16
GE = 128 * J
NG = -(-E // GE)
LAST = E - GE
DUP = (NG * GE - E) // J
assert DUP * J == NG * GE - E and NG % 2 == 0 and NP * NT == N
WIN = 128
NPAD = N + 150
BIG = 1e30
FAR = 1e6

NX = 48
assert NX >= N // WIN and NX % 2 == 0
DUMMY = N

TAB = C + H + 1
TW = TAB + H
ST = TAB + C


def gnn_kernel(nc, x, src, dst, attr, W, att_src, att_dst, bias0, We, be, W1, b1, W2, b2, out):
    ctx = ExitStack()
    with ctx:
        def sb(name, shape, dt=FP32):
            return ctx.enter_context(nc.sbuf_tensor(name, shape, dt))

        def sem(name):
            return ctx.enter_context(nc.semaphore(name))

        def dram(name, shape):
            return nc.dram_tensor(name, shape, FP32, kind="Internal").ap()

        table0 = dram("table0", [N, TAB])
        table1 = dram("table1", [N, C])
        dlogit = dram("dlogit", [NPAD, H])
        peak = dram("peak", [NPAD, H])
        sums0 = dram("sums0", [NPAD, ST])
        sums1 = dram("sums1", [NPAD, C])

        xs = sb("xs", [128, NT, C])
        tab = sb("tab", [128, NT, TW])
        big = sb("big", [128, NT * ST])
        V = [big[:, b * J * TAB:(b + 1) * J * TAB].rearrange("p (j c) -> p j c", c=TAB) for b in range(2)]
        o = 2 * J * TAB
        AT = [big[:, o + b * J * C:o + (b + 1) * J * C].rearrange("p (j c) -> p j c", c=C) for b in range(2)]
        o += 2 * J * C
        SEL = [big[:, o + b * J * WIN:o + (b + 1) * J * WIN].rearrange("p (j w) -> p j w", w=WIN)
               for b in range(2)]
        assert o + 2 * J * WIN <= NT * ST
        allsum = big[:, :].rearrange("p (t c) -> p t c", c=ST)
        zin = big[:, 0:NT * C].rearrange("p (t c) -> p t c", c=C)
        selT = sb("selT", [128, J * 128])
        dsti = sb("dsti", [128, NG, J], INT32)
        dd = sb("dd", [128, NG, J])
        drel = sb("drel", [128, NG, J])
        cont = sb("cont", [128, NG, J])
        isl = sb("isl", [128, NG, J])
        cin = sb("cin", [128, NG])
        thru = sb("thru", [128, NG])
        firsts = sb("firsts", [128, NG])
        lasts = sb("lasts", [128, NG])
        basei = sb("basei", [1, NG], INT32)
        idx = [sb(f"idx{b}", [128, J], INT32) for b in range(2)]
        iotaf = sb("iotaf", [128, 128])
        ident = sb("ident", [128, 128])
        shp = sb("shp", [128, 128])
        shn = sb("shn", [128, 128])
        pick = [sb(f"pick{i}", [128, 128]) for i in range(3)]
        edgefix = sb("edgefix", [128, 2])
        wcat = sb("wcat", [128, TW])
        wT = sb("wT", [128, 128])
        weT = sb("weT", [128, 128])
        attm = sb("attm", [128, 2 * H + 1])
        wes = sb("wes", [128, C])
        w1a = sb("w1a", [128, C])
        w1b = sb("w1b", [128, C])
        wew = sb("wew", [128, C])
        w2s = sb("w2s", [128, C])
        bes = sb("bes", [128, 1])
        beb = sb("beb", [128, 128])
        bew = sb("bew", [128, C])
        b0s = sb("b0s", [128, C])
        b2s = sb("b2s", [128, C])
        b1s = sb("b1s", [128, 1])
        init = sb("init", [128, ST - C])
        stat = sb("stat", [128, NT, 6])
        lnw = sb("lnw", [128, 4, NT])
        rstd = sb("rstd", [128, NT])
        nmr = sb("nmr", [128, NT])
        epsc = sb("epsc", [128, 1])
        rden = sb("rden", [128, NT, H])
        hb = [sb(f"hb{b}", [128, 2, 128]) for b in range(2)]
        hT = [sb(f"hT{b}", [128, 2, 128]) for b in range(2)]
        cont4 = sb("cont4", [128, H, J])
        logit = sb("logit", [128, H, J])
        pre1 = sb("pre1", [128, H, J])
        pre2 = sb("pre2", [128, H, J])
        thru4 = [sb(f"thru4{b}", [128, H]) for b in range(2)]
        thruT = sb("thruT", [H, 128])
        tails = sb("tails", [H, 129])
        peaks = sb("peaks", [128, J, H + 1])
        pen = sb("pen", [128, 1])
        newold = [sb(f"newold{b}", [128, 2, H]) for b in range(2)]
        node = [sb(f"node{b}", [128, 3 * H]) for b in range(2)]
        fold = [sb(f"fold{b}", [128, H]) for b in range(2)]
        lin = sb("lin", [128, J, H])
        lre = sb("lre", [128, J, H])
        state = sb("state", [128, ST])
        nu = sb("nu", [128, 2 * H])
        fd = sb("fd", [128, H])

        def bank(name):
            return ctx.enter_context(nc.psum_tensor(name, [128, 512], FP32))
        pv = [bank(f"pv{b}") for b in range(2)]
        pa = [bank(f"pa{b}") for b in range(2)]
        pt = [bank(f"pt{b}") for b in range(2)]
        pc = bank("pc")
        pm = bank("pm")
        iotap = pc[:, 0:128]
        tailT = pm[0:H, 0:128]
        thruP = pm[0:H, 128:256]
        cback = pm[:, 256:256 + H]
        mg = pm[:, 264:264 + H + 1]
        lk = pm[:, 272:272 + 2 * H * J].rearrange("p (j c) -> p j c", c=2 * H)
        wps = pm[:, 400:400 + H * J].rearrange("p (j c) -> p j c", c=H)

        S = {}

        def s(name):
            if name not in S:
                S[name] = sem(name)
            return S[name]

        names = """x_in idx_dst consts_in ones_done ident_done iota_p
            pool_c w_t w_tc w_aux w_auxc prep d_f shifted masks drel_done base_i
            stats ln_a ln_sq ln_b h_ready h_tr h_trc h_mm h_ev tab_done pad_z tab_out pad_out
            idx0 idx1 gat0 gat1 attr0 attr1 g_started
            st_load m_store s_load s_store
            sel_b cont_b log_b pre1_b tailT_b thruT_b tails_b cback_b carry_b pre2_b pk_b pkl_b mg_b pen_b
            mnew_b nu_b node_b fd_b fold_b sttr stcp look lin_b lre_b zs_b zm_b w_b wp_b vw_b am_b vm_b
            ms_b mt_b mu_b merged
            sum_in den_r o_n o_b o_r x1_done ln2 y_ready tab1_done tab1_out zpad
            thru_c thru4_b chain beb_done i20 i21 g20 g21 sel2 vm2 z_load z_add z_store g2_started
            z_in zc_r zc_t zc_u zc_m zc_o out_w b2add""".split()
        for n_ in names:
            s(n_)

        block = ctx.enter_context(nc.Block())

        def nodes(ap, width_from, width_to):
            return ap[0:N, width_from:width_to].rearrange("(p t) c -> p t c", t=NT)

        def after(eng, sm, n, lag=0):
            if isinstance(n, int) and n - lag < 0:
                return
            eng.wait_ge(sm, n + (1 - lag))

        def after_dma(eng, sm, count):
            if isinstance(count, int) and count <= 0:
                return
            eng.wait_ge(sm, count * 16)

        def pairs(eng, body, first, count, peel_last=False):
            lo = first
            if first == 0:
                for b in range(2):
                    body(b, b, 0)
                lo = 1
            hi = first + count - (1 if peel_last else 0)
            with eng.Fori(lo, hi) as it:
                for b in range(2):
                    body(it * 2 + b, b, it)
            if peel_last:
                for b in range(2):
                    body(2 * hi + b, b, hi)

        @block.sync
        def _(sp):
            for lo, hi in ((0, SPLIT), (SPLIT, NP)):
                sp.dma_start(xs[lo:hi, :, :], nodes(x, 0, C)[lo:hi]).then_inc(s("x_in"), 16)
            sp.wait_ge(s("prep"), 1)
            sp.dma_start(wcat[:, 0:C], W).then_inc(s("consts_in"), 16)
            for h in range(H):
                sp.dma_start(attm[h * F:(h + 1) * F, h:h + 1],
                             att_src[h, :].rearrange("(f a) -> f a", a=1)).then_inc(s("consts_in"), 16)
                sp.dma_start(attm[h * F:(h + 1) * F, H + 1 + h:H + 2 + h],
                             att_dst[h, :].rearrange("(f a) -> f a", a=1)).then_inc(s("consts_in"), 16)
            sp.dma_start(wes[:, :], We).then_inc(s("consts_in"), 16)
            sp.dma_start(w1a[:, :], W1[0:C, :]).then_inc(s("consts_in"), 16)
            sp.dma_start(w1b[:, :], W1[C:2 * C, :]).then_inc(s("consts_in"), 16)
            sp.dma_start(w2s[:, :], W2).then_inc(s("consts_in"), 16)
            sp.dma_start(bes[:, :], be.rearrange("(p a) -> p a", a=1)).then_inc(s("consts_in"), 16)
            sp.dma_start(b1s[:, :], b1.rearrange("(p a) -> p a", a=1)).then_inc(s("consts_in"), 16)
            sp.dma_start(b0s[:, :], bias0.rearrange("(a n) -> a n", a=1).to_broadcast([128, C]))\
                .then_inc(s("consts_in"), 16)
            sp.dma_start(b2s[:, :], b2.rearrange("(a n) -> a n", a=1).to_broadcast([128, C]))\
                .then_inc(s("consts_in"), 16)
            sp.dma_start(dsti[:, 0:NG - 1, :],
                         dst[0:(NG - 1) * GE].rearrange("(g p j) -> p g j", p=128, j=J))\
                .then_inc(s("idx_dst"), 16)
            sp.dma_start(dsti[:, NG - 1, :], dst[LAST:E].rearrange("(p j) -> p j", j=J))\
                .then_inc(s("idx_dst"), 16)

            sp.wait_ge(s("pad_z"), 1)
            pads = NPAD - N
            zero = init[:, H:H + 1]
            for ap, wd in ((dlogit, H), (peak, H), (sums0, ST), (sums1, C)):
                rows = ap[N:NPAD, :].rearrange("(p q) c -> p (q c)", p=75)
                n_el = pads // 75 * wd
                done = 0
                while done < n_el:
                    k = min(n_el - done, ST - C - H)
                    sp.dma_start(rows[:, done:done + k], init[0:75, H:H + k]).then_inc(s("pad_out"), 16)
                    done += k

            sp.wait_ge(s("tab_done"), 1)
            for lo, hi in ((0, SPLIT), (SPLIT, NP)):
                for ap, to, frm, wd in ((table0, 0, 0, TAB), (dlogit, 0, TAB, H), (peak, 0, C, H),
                                        (sums0, 0, 0, C)):
                    sp.dma_start(nodes(ap, to, to + wd)[lo:hi], tab[lo:hi, :, frm:frm + wd])\
                        .then_inc(s("tab_out"), 16)
                sp.dma_start(nodes(sums0, C, ST)[lo:hi],
                             init[lo:hi, :].rearrange("p (a c) -> p a c", a=1).to_broadcast([hi - lo, NT, ST - C]))\
                    .then_inc(s("tab_out"), 16)

            def load_edges(n, b, it, start):
                after_dma(sp, s(f"gat{b}"), it * J)
                sp.dma_start(idx[b][:, :], src[bass.DynSlice(start, GE)].rearrange("(p j) -> p j", j=J))\
                    .then_inc(s(f"idx{b}"), 16)
                after(sp, s("am_b"), n, 2)
                sp.dma_start(AT[b], attr[bass.DynSlice(start, GE), :].rearrange("(p j) c -> p j c", j=J))\
                    .then_inc(s(f"attr{b}"), 16)

            def load_peak(n, b, base):
                after_dma(sp, s("m_store"), n)
                sp.dma_start(newold[b][:, 1, :], peak[bass.DynSlice(base, WIN), :]).then_inc(s("st_load"), 16)
                sp.dma_start(node[b][:, 0:H], dlogit[bass.DynSlice(base, WIN), :]).then_inc(s("st_load"), 16)

            def store_peak(n, b, base):
                after(sp, s("mnew_b"), n)
                sp.dma_start(peak[bass.DynSlice(base, WIN), :], newold[b][:, 0, :]).then_inc(s("m_store"), 16)

            def update_sums(n, base):
                after_dma(sp, s("s_store"), n)
                sp.dma_start(state[:, :], sums0[bass.DynSlice(base, WIN), :]).then_inc(s("s_load"), 16)
                after(sp, s("merged"), n)
                sp.dma_start(sums0[bass.DynSlice(base, WIN), :], state[:, :]).then_inc(s("s_store"), 16)

            sp.wait_ge(s("base_i"), 1)
            sp.wait_ge(s("pad_out"), 16 * PADS)
            sp.wait_ge(s("tab_out"), 16 * 10)

            def base_of(g):
                return sp.value_load(basei[0:1, bass.DynSlice(g, 1)], min_val=0, max_val=N)

            def item(n, b, it):
                if isinstance(n, int) and n < 2:
                    load_edges(n, b, it, n * GE)
                base = base_of(n)
                load_peak(n, b, base)
                if not (isinstance(n, int) and n == 0):
                    update_sums(n - 1, base_of(n - 1))
                store_peak(n, b, base)
                if isinstance(n, int) and n + 2 >= NG - 1:
                    if n + 2 == NG - 1:
                        load_edges(n + 2, b, it + 1, LAST)
                elif isinstance(n, int) and n + 2 >= NG:
                    pass
                else:
                    load_edges(n + 2, b, it + 1, (n + 2) * GE)

            for b in range(2):
                item(b, b, 0)
            with sp.Fori(1, NG // 2 - 2) as it:
                for b in range(2):
                    item(it * 2 + b, b, it)
            for it in range(NG // 2 - 2, NG // 2):
                for b in range(2):
                    item(it * 2 + b, b, it)
            update_sums(NG - 1, base_of(NG - 1))

            sp.wait_ge(s("s_store"), 16 * NG)
            for lo, hi in ((0, SPLIT), (SPLIT, NP)):
                sp.dma_start(allsum[lo:hi], nodes(sums0, 0, ST)[lo:hi]).then_inc(s("sum_in"), 16)
            sp.wait_ge(s("tab1_done"), 1)
            for lo, hi in ((0, SPLIT), (SPLIT, NP)):
                sp.dma_start(nodes(table1, 0, C)[lo:hi], tab[lo:hi, :, 0:C]).then_inc(s("tab1_out"), 16)
                sp.dma_start(nodes(sums1, 0, C)[lo:hi], tab[lo:hi, :, 0:C]).then_inc(s("tab1_out"), 16)

            def load_idx(n, b, it, start):
                after_dma(sp, s(f"g2{b}"), it * J)
                sp.dma_start(idx[b][:, :], src[bass.DynSlice(start, GE)].rearrange("(p j) -> p j", j=J))\
                    .then_inc(s(f"i2{b}"), 16)

            def update_z(n, base):
                after_dma(sp, s("z_store"), n)
                sp.dma_start(state[:, 0:C], sums1[bass.DynSlice(base, WIN), :]).then_inc(s("z_load"), 16)
                after(sp, s("z_add"), n)
                sp.dma_start(sums1[bass.DynSlice(base, WIN), :], state[:, 0:C]).then_inc(s("z_store"), 16)

            sp.wait_ge(s("tab1_out"), 16 * 4)
            for b in range(2):
                load_idx(b, b, 0, b * GE)

            def item2(n, b, it):
                if isinstance(n, int) and n + 2 >= NG - 1:
                    if n + 2 == NG - 1:
                        load_idx(n + 2, b, it + 1, LAST)
                elif not (isinstance(n, int) and n + 2 >= NG):
                    load_idx(n + 2, b, it + 1, (n + 2) * GE)
                update_z(n, base_of(n))

            for b in range(2):
                item2(b, b, 0)
            with sp.Fori(1, NG // 2 - 2) as it:
                for b in range(2):
                    item2(it * 2 + b, b, it)
            for it in range(NG // 2 - 2, NG // 2):
                for b in range(2):
                    item2(it * 2 + b, b, it)
            sp.wait_ge(s("z_store"), 16 * NG)
            for lo, hi in ((0, SPLIT), (SPLIT, NP)):
                sp.dma_start(zin[lo:hi], nodes(sums1, 0, C)[lo:hi]).then_inc(s("z_in"), 16)
            sp.wait_ge(s("zc_o"), NT)
            for lo, hi in ((0, SPLIT), (SPLIT, NP)):
                sp.dma_start(nodes(out, 0, C)[lo:hi], tab[lo:hi, :, 0:C]).then_inc(s("out_w"), 16)
            sp.wait_ge(s("out_w"), 32)

        @block.gpsimd
        def _(pool):
            pool.memset(attm[:, :], 0.0).then_inc(s("prep"), 1)
            pool.memset(wcat[:, C:TW], 0.0).then_inc(s("pool_c"), 1)
            pool.memset(init[:, 0:H], 1.0).then_inc(s("pool_c"), 1)
            pool.memset(init[:, H:ST - C], 0.0).then_inc(s("pool_c"), 1)
            pool.wait_ge(s("pool_c"), 3)
            pool.iota(iotaf[:, :], [[1, 128]], base=0, channel_multiplier=0,
                      allow_small_or_imprecise_dtypes=True).then_inc(s("pad_z"), 1)
            tiles = [(ident, 0, 1, [[-1, 128]]), (shp, 1, 1, [[-1, 128]]), (shn, -1, 1, [[-1, 128]]),
                     (pick[0], 0, 1, [[0, 128]]), (pick[1], -127, 1, [[0, 128]]), (pick[2], -DUP, 1, [[0, 128]])]
            for tl, _, _, _ in tiles:
                pool.memset(tl[:, :], 0.0).then_inc(s("pool_c"), 1)
            pool.memset(edgefix[:, :], 0.0).then_inc(s("pool_c"), 1)
            pool.memset(epsc[:, :], EPS).then_inc(s("pool_c"), 1)
            pool.memset(tails[:, :], -BIG).then_inc(s("pool_c"), 1)
            pool.wait_ge(s("pool_c"), 12)
            for tl, base, cm, pat in tiles:
                pool.affine_select(out=tl[:, :], in_=tl[:, :], compare_op=ALU.not_equal, fill=1.0,
                                   base=base, pattern=pat, channel_multiplier=cm).then_inc(s("pool_c"), 1)
            for c, base in ((0, 0), (1, -127)):
                pool.affine_select(out=edgefix[:, c:c + 1], in_=edgefix[:, c:c + 1], compare_op=ALU.not_equal,
                                   fill=-1.0, base=base, pattern=[[0, 1]], channel_multiplier=1)\
                    .then_inc(s("pool_c"), 1)

            def gather(b, it, rows, table, gat, ix, started):
                pool.wait_ge(s(f"{ix}{b}"), it * 16 + 16)
                pool.sem_inc(s(started), 1)
                for j in range(J):
                    pool.indirect_dma_start(
                        out=V[b][:, j, 0:rows], out_offset=None, in_=table,
                        in_offset=bass.IndirectOffsetOnAxis(ap=idx[b][:, j:j + 1], axis=0))\
                        .then_inc(s(f"{gat}{b}"), 16)

            pool.wait_ge(s("tab_out"), 16 * 10)

            def item(n, b, it):
                after(pool, s("vm_b"), n, 2)
                gather(b, it, TAB, table0, "gat", "idx", "g_started")
            pairs(pool, item, 0, NG // 2)

            pool.wait_ge(s("tab1_out"), 16 * 4)

            def item2(n, b, it):
                after(pool, s("vm2"), n, 2)
                gather(b, it, C, table1, "g2", "i2", "g2_started")
            pairs(pool, item2, 0, NG // 2)

        @block.scalar
        def _(act):
            def a(out_, in_, func, name, **kw):
                return nc.scalar.activation(out_, in_, func, **kw).then_inc(s(name), 1)

            act.wait_ge(s("pad_z"), 1)
            a(iotap, iotaf[:, :], ACT.Copy, "iota_p")
            act.wait_ge(s("w_t"), 2)
            a(wT[:, :], pt[0][:, 0:128], ACT.Copy, "w_tc")
            a(weT[:, :], pt[0][:, 128:256], ACT.Copy, "w_tc")
            act.wait_ge(s("w_aux"), 3)
            a(wcat[:, C:TW], pt[1][:, 0:2 * H + 1], ACT.Copy, "w_auxc")
            a(wew[:, :], pt[1][:, 128:256], ACT.Copy, "w_auxc")
            a(bew[:, :], pt[1][:, 256:384], ACT.Copy, "w_auxc")

            def standard_deviation(k):
                act.wait_ge(s("ln_a"), k)
                a(lnw[0:NP, 1, :], lnw[0:NP, 0, :], ACT.Sqrt, "ln_sq", bias=epsc[0:NP, 0:1])

            def normalised(t, b, k, lag_name):
                a(hb[b][0:NP, 0, :], xs[0:NP, bass.DynSlice(t, 1), :].rearrange("p a c -> p (a c)"),
                  ACT.Relu, "h_ready", scale=rstd[0:NP, bass.DynSlice(t, 1)],
                  bias=nmr[0:NP, bass.DynSlice(t, 1)])

            standard_deviation(1)
            act.wait_ge(s("ln_b"), 1)

            def node0(t, b, it):
                after(act, s("h_tr"), t, 2)
                normalised(t, b, 0, None)
            pairs(act, node0, 0, NT // 2)

            def item(n, b, it):
                n4 = n * 4
                after(act, s("thruT_b"), n)
                if not (isinstance(n, int) and n == 0):
                    act.wait_ge(s("tails_b"), n)
                a(thruT[:, :], thruP, ACT.Copy, "thru_c")
                after(act, s("look"), n, 1)
                for r in range(4):
                    act.wait_ge(s("sttr"), n4 + (r + 1))
                    a(selT[:, r * 512:(r + 1) * 512], pt[r % 2][:, :], ACT.Copy, "stcp")
                after(act, s("fd_b"), n)
                a(fold[b][:, :], fd[:, :], ACT.Exp, "fold_b")
                after(act, s("zm_b"), n)
                a(V[b][:, :, C:C + H], lre[:, :, :], ACT.Exp, "w_b")
                a(wps, lre[:, :, :], ACT.Exp, "wp_b")
            pairs(act, item, 0, NG // 2)

            standard_deviation(2)
            act.wait_ge(s("ln_b"), 2)

            def node1(t, b, it):
                n = t + NT
                act.wait_ge(s("h_tr"), n - 1)
                normalised(t, b, 1, None)
                a(hb[b][0:NP, 1, :], allsum[0:NP, bass.DynSlice(t, 1), TAB:ST].rearrange("p a c -> p (a c)"),
                  ACT.Copy, "y_ready")
            pairs(act, node1, 0, NT // 2)

            act.wait_ge(s("z_in"), 32)

            def node2(t, b, it):
                after(act, s("zc_t"), t, 2)
                a(hb[b][0:NP, 0, :], zin[0:NP, bass.DynSlice(t, 1), :].rearrange("p a c -> p (a c)"),
                  ACT.Copy, "zc_r")
                after(act, s("zc_t"), t)
                a(hT[b][:, 0, 0:NP], pt[b][:, 0:NP], ACT.Relu, "zc_u", bias=b1s[:, 0:1])
            pairs(act, node2, 0, NT // 2)

        @block.tensor
        def _(pe):
            pe.wait_ge(s("pool_c"), 20)
            pe.wait_ge(s("consts_in"), 16 * CONSTS)
            nc.tensor.transpose(pt[0][:, 0:128], wcat[:, 0:C], ident[:, :]).then_inc(s("w_t"), 1)
            nc.tensor.transpose(pt[0][:, 128:256], wes[:, :], ident[:, :]).then_inc(s("w_t"), 1)
            pe.wait_ge(s("w_tc"), 2)
            nc.tensor.matmul(pt[1][:, 0:2 * H + 1], wT[:, :], attm[:, :], start=True, stop=True)\
                .then_inc(s("w_aux"), 1)
            nc.tensor.matmul(pt[1][:, 128:256], weT[:, :], w1b[:, :], start=True, stop=True)\
                .then_inc(s("w_aux"), 1)
            pe.wait_ge(s("beb_done"), 1)
            nc.tensor.matmul(pt[1][:, 256:384], beb[:, :], w1b[:, :], start=True, stop=True)\
                .then_inc(s("w_aux"), 1)
            pe.wait_ge(s("d_f"), 2)
            nc.tensor.matmul(pa[0][:, 0:NG], shp[:, :], dd[:, :, J - 1], start=True, stop=True)\
                .then_inc(s("shifted"), 1)
            nc.tensor.matmul(pa[0][:, 128:128 + NG], shn[:, :], dd[:, :, 0], start=True, stop=True)\
                .then_inc(s("shifted"), 1)
            nc.tensor.matmul(pa[0][:, 256:256 + NG - 1], pick[0][:, :], dd[:, 0:NG - 1, 0], start=True, stop=True)\
                .then_inc(s("shifted"), 1)
            nc.tensor.matmul(pa[0][:, 256 + NG - 1:256 + NG], pick[2][:, :], dd[:, NG - 1, 0:1],
                             start=True, stop=True).then_inc(s("shifted"), 1)
            nc.tensor.matmul(pa[0][:, 384:384 + NG], pick[1][:, :], dd[:, :, J - 1], start=True, stop=True)\
                .then_inc(s("shifted"), 1)

            pe.wait_ge(s("w_auxc"), 3)

            def node0(t, b, it):
                after(pe, s("h_ready"), t)
                after(pe, s("h_trc"), t, 2)
                nc.tensor.transpose(pt[b][:, 0:NP], hb[b][0:NP, 0, :], ident[0:NP, 0:NP]).then_inc(s("h_tr"), 1)
                after(pe, s("h_trc"), t)
                after(pe, s("h_ev"), t, 2)
                nc.tensor.matmul(pv[b][0:NP, 0:TW], hT[b][:, 0, 0:NP], wcat[:, :], start=True, stop=True)\
                    .then_inc(s("h_mm"), 1)
            pairs(pe, node0, 0, NT // 2)

            def item(n, b, it):
                n4 = n * 4
                after(pe, s("thru4_b"), n)
                nc.tensor.transpose(thruP, thru4[b][:, :], ident[:, :]).then_inc(s("thruT_b"), 1)
                after(pe, s("sel_b"), n)
                for r in range(4):
                    if not (isinstance(n, int) and n4 + r - 1 <= 0):
                        pe.wait_ge(s("stcp"), n4 + (r - 1))
                    for q in range(4):
                        ins = nc.tensor.transpose(pt[r % 2][:, q * 128:(q + 1) * 128],
                                                  SEL[b][:, 4 * r + q, :], ident[:, :])
                    ins.then_inc(s("sttr"), 1)
                pe.wait_ge(s(f"attr{b}"), it * 16 + 16)
                after(pe, s("merged"), n, 2)
                for j in range(J):
                    ins = nc.tensor.matmul(pa[b][:, 0:C], SEL[b][:, j, :], AT[b][:, j, :],
                                           start=(j == 0), stop=(j == J - 1))
                ins.then_inc(s("am_b"), 1)
                after(pe, s("pre1_b"), n)
                nc.tensor.transpose(tailT, pre1[:, :, J - 1], ident[:, :]).then_inc(s("tailT_b"), 1)
                after(pe, s("tails_b"), n)
                nc.tensor.matmul(cback, tails[:, 0:128], ident[0:H, 0:H], start=True, stop=True).then_inc(s("cback_b"), 1)
                after(pe, s("pkl_b"), n)
                after(pe, s("pk_b"), n)
                for j in range(J):
                    ins = nc.tensor.matmul(mg, SEL[b][:, j, :], peaks[:, j, :],
                                           start=(j == 0), stop=(j == J - 1))
                ins.then_inc(s("mg_b"), 1)
                after(pe, s("node_b"), n)
                pe.wait_ge(s("stcp"), n4 + 4)
                for j in range(J):
                    ins = nc.tensor.matmul(lk[:, j, :], selT[:, j * 128:(j + 1) * 128], node[b][:, 0:2 * H],
                                           start=True, stop=True)
                ins.then_inc(s("look"), 1)
                after(pe, s("vw_b"), n)
                after(pe, s("w_b"), n)
                for j in range(J):
                    ins = nc.tensor.matmul(pv[b][:, 0:TAB], SEL[b][:, j, :], V[b][:, j, :],
                                           start=(j == 0), stop=(j == J - 1))
                ins.then_inc(s("vm_b"), 1)

            pairs(pe, item, 0, NG // 2)

            def node1(t, b, it):
                after(pe, s("y_ready"), t)
                n = t + NT
                pe.wait_ge(s("h_ready"), n + 1)
                pe.wait_ge(s("h_trc"), n - 1)
                nc.tensor.transpose(pt[b][:, 0:NP], hb[b][0:NP, 0, :], ident[0:NP, 0:NP])
                nc.tensor.transpose(pt[b][:, 128:128 + NP], hb[b][0:NP, 1, :], ident[0:NP, 0:NP])\
                    .then_inc(s("h_tr"), 1)
                pe.wait_ge(s("h_trc"), n + 1)
                pe.wait_ge(s("h_ev"), n - 1)
                nc.tensor.matmul(pv[b][0:NP, 0:C], hT[b][:, 0, 0:NP], w1a[:, :], start=True, stop=False)
                nc.tensor.matmul(pv[b][0:NP, 0:C], hT[b][:, 1, 0:NP], wew[:, :], start=False, stop=True)\
                    .then_inc(s("h_mm"), 1)
            pairs(pe, node1, 0, NT // 2)

            def item2(n, b, it):
                after(pe, s("sel2"), n)
                pe.wait_ge(s(f"g2{b}"), it * 16 * J + 16 * J)
                after(pe, s("z_add"), n, 2)
                for j in range(J):
                    ins = nc.tensor.matmul(pv[b][:, 0:C], SEL[b][:, j, :], V[b][:, j, 0:C],
                                           start=(j == 0), stop=(j == J - 1))
                ins.then_inc(s("vm2"), 1)
            pairs(pe, item2, 0, NG // 2)

            def node2(t, b, it):
                after(pe, s("zc_r"), t)
                after(pe, s("zc_u"), t, 2)
                nc.tensor.transpose(pt[b][:, 0:NP], hb[b][0:NP, 0, :], ident[0:NP, 0:NP]).then_inc(s("zc_t"), 1)
                after(pe, s("zc_u"), t)
                after(pe, s("zc_o"), t, 2)
                nc.tensor.matmul(pv[b][0:NP, 0:C], hT[b][:, 0, 0:NP], w2s[:, :], start=True, stop=True)\
                    .then_inc(s("zc_m"), 1)
            pairs(pe, node2, 0, NT // 2)

        @block.vector
        def _(dve):
            v = nc.vector
            count = [0]

            def link(ins):
                count[0] += 1
                ins.then_inc(s("chain"), 1)
                dve.wait_ge(s("chain"), count[0])

            def row(t3, t, lo, hi):
                return t3[0:NP, bass.DynSlice(t, 1), lo:hi].rearrange("p a c -> p (a c)")

            def layernorm(k, off):
                with dve.Fori(0, NT // 5) as it:
                    for q in range(5):
                        t = it * 5 + q
                        v.bn_stats(row(stat, t, 0, 6), row(xs, t, 0, C)).then_inc(s("stats"), 1)
                dve.wait_ge(s("stats"), k * NT)
                m_e, q_e = stat[0:NP, :, 1], stat[0:NP, :, 2]
                m_o, q_o = stat[0:NP, :, 4], stat[0:NP, :, 5]
                w0, w1, w2, w3 = (lnw[0:NP, i, :] for i in range(4))
                link(v.tensor_tensor(w2, m_e, m_o, ALU.subtract))
                link(v.tensor_tensor(w2, w2, w2, ALU.mult))
                link(v.tensor_tensor(w3, q_e, q_o, ALU.add))
                link(v.tensor_scalar(w2, w2, 0.25, None, ALU.mult))
                v.scalar_tensor_tensor(out=w0, in0=w3, scalar=1.0 / C, in1=w2, op0=ALU.mult,
                                       op1=ALU.add).then_inc(s("ln_a"), 1)
                dve.wait_ge(s("ln_a"), k)
                link(v.tensor_tensor(w3, m_e, m_o, ALU.add))
                dve.wait_ge(s("ln_sq"), k)
                link(v.reciprocal(rstd[0:NP, :], w1))
                v.scalar_tensor_tensor(out=nmr[0:NP, :], in0=w3, scalar=-0.5, in1=rstd[0:NP, :],
                                       op0=ALU.mult, op1=ALU.mult).then_inc(s("ln_b"), 1)

            dve.wait_ge(s("consts_in"), 16 * CONSTS)
            v.tensor_copy(beb[:, :], bes[:, 0:1].to_broadcast([128, 128])).then_inc(s("beb_done"), 1)
            dve.wait_ge(s("x_in"), 32)
            layernorm(1, 0)
            dve.wait_ge(s("idx_dst"), 32)
            link(v.tensor_copy(dd[:, :, :], dsti[:, :, :]))
            v.tensor_scalar(dd[0:DUP, NG - 1, :], dd[0:DUP, NG - 1, :], FAR, None, ALU.add).then_inc(s("d_f"), 2)
            dve.wait_ge(s("d_f"), 2)
            dve.wait_ge(s("shifted"), 5)
            dve.wait_ge(s("pool_c"), 20)
            prev, nxt = pa[0][:, 0:NG], pa[0][:, 128:128 + NG]
            v.tensor_copy(firsts[:, :], pa[0][:, 256:256 + NG]).then_inc(s("masks"), 1)
            v.tensor_copy(basei[0:1, :], pa[0][0:1, 256:256 + NG]).then_inc(s("base_i"), 1)
            v.tensor_copy(lasts[:, :], pa[0][:, 384:384 + NG]).then_inc(s("masks"), 1)
            v.tensor_tensor(isl[:, :, 0:J - 1], dd[:, :, 0:J - 1], dd[:, :, 1:J], ALU.not_equal)\
                .then_inc(s("masks"), 1)
            v.scalar_tensor_tensor(out=isl[:, :, J - 1], in0=nxt, scalar=edgefix[:, 1:2], in1=dd[:, :, J - 1],
                                   op0=ALU.add, op1=ALU.not_equal).then_inc(s("masks"), 1)
            v.tensor_tensor(cont[:, :, 1:J], dd[:, :, 0:J - 1], dd[:, :, 1:J], ALU.not_equal)\
                .then_inc(s("masks"), 1)
            v.memset(cont[:, :, 0:1], 1.0).then_inc(s("masks"), 1)
            v.scalar_tensor_tensor(out=cin[:, :], in0=prev, scalar=edgefix[:, 0:1], in1=dd[:, :, 0],
                                   op0=ALU.add, op1=ALU.not_equal).then_inc(s("masks"), 1)
            v.scalar_tensor_tensor(out=thru[:, :], in0=prev, scalar=edgefix[:, 0:1], in1=dd[:, :, J - 1],
                                   op0=ALU.add, op1=ALU.not_equal).then_inc(s("masks"), 1)
            dve.wait_ge(s("masks"), 8)
            for m in (cont[:, :, :], cin[:, :], thru[:, :]):
                v.tensor_scalar(m, m, -BIG, None, ALU.mult).then_inc(s("masks"), 1)
            v.tensor_tensor(drel[:, :, :], dd[:, :, :], firsts[:, :].rearrange("p (g a) -> p g a", a=1)
                            .to_broadcast([128, NG, J]), ALU.subtract).then_inc(s("masks"), 1)
            dve.wait_ge(s("masks"), 12)

            def node0(t, b, it):
                after(dve, s("h_tr"), t)
                after(dve, s("h_mm"), t, 2)
                v.tensor_copy(hT[b][:, 0, 0:NP], pt[b][:, 0:NP]).then_inc(s("h_trc"), 1)
                after(dve, s("h_mm"), t)
                v.tensor_copy(row(tab, t, 0, TW), pv[b][0:NP, 0:TW]).then_inc(s("h_ev"), 1)
            pairs(dve, node0, 0, NT // 2)
            dve.wait_ge(s("h_ev"), NT)
            v.memset(tab[0:NP, :, TAB - 1:TAB], 1.0).then_inc(s("tab_done"), 1)

            dve.wait_ge(s("iota_p"), 1)

            def select(n, b, name):
                v.tensor_tensor(SEL[b], iotap.rearrange("p (a w) -> p a w", a=1).to_broadcast([128, J, WIN]),
                                drel[:, bass.DynSlice(n, 1), :].rearrange("p a (j c) -> p (a j) c", c=1)
                                .to_broadcast([128, J, WIN]), ALU.is_equal).then_inc(s(name), 1)

            def merge(n, b):
                dve.wait_ge(s("s_load"), n * 16 + 16)
                after(dve, s("fold_b"), n)
                st4 = state[:, 0:C].rearrange("p (h f) -> p h f", f=F)
                v.tensor_tensor(st4, st4, fold[b][:, :].rearrange("p (h a) -> p h a", a=1)
                                .to_broadcast([128, H, F]), ALU.mult).then_inc(s("ms_b"), 1)
                v.tensor_tensor(state[:, C:C + H], state[:, C:C + H], fold[b][:, :], ALU.mult)\
                    .then_inc(s("mt_b"), 1)
                after(dve, s("am_b"), n)
                v.tensor_tensor(state[:, TAB:ST], state[:, TAB:ST], pa[b][:, 0:C], ALU.add)\
                    .then_inc(s("mu_b"), 1)
                after(dve, s("vm_b"), n)
                after(dve, s("ms_b"), n)
                after(dve, s("mt_b"), n)
                after(dve, s("mu_b"), n)
                v.tensor_tensor(state[:, 0:TAB], state[:, 0:TAB], pv[b][:, 0:TAB], ALU.add)\
                    .then_inc(s("merged"), 1)

            def item(n, b, it):
                after(dve, s("vm_b"), n, 2)
                select(n, b, "sel_b")
                after(dve, s("thruT_b"), n, 1)
                v.tensor_copy(thru4[b][:, :], thru[:, bass.DynSlice(n, 1)].to_broadcast([128, H]))\
                    .then_inc(s("thru4_b"), 1)
                v.tensor_copy(cont4[:, :, :], cont[:, bass.DynSlice(n, 1), :].to_broadcast([128, H, J]))\
                    .then_inc(s("cont_b"), 1)
                if not (isinstance(n, int) and n == 0):
                    merge(n - 1, 1 - b)
                dve.wait_ge(s(f"gat{b}"), it * 16 * J + 16 * J)
                v.tensor_copy(logit[:, :, :], V[b][:, :, C:C + H].rearrange("p j h -> p h j"))\
                    .then_inc(s("log_b"), 1)
                after(dve, s("cont_b"), n)
                after(dve, s("log_b"), n)
                flat = "p h j -> p (h j)"
                v.tensor_tensor_scan(pre1[:, :, :].rearrange(flat), cont4[:, :, :].rearrange(flat),
                                     logit[:, :, :].rearrange(flat), -BIG, ALU.add, ALU.max)\
                    .then_inc(s("pre1_b"), 1)
                after(dve, s("thru_c"), n)
                after(dve, s("tailT_b"), n)
                v.tensor_tensor_scan(tails[:, 1:129], thruT[:, :], tailT, -BIG, ALU.add, ALU.max)\
                    .then_inc(s("tails_b"), 1)
                after(dve, s("cback_b"), n)
                v.scalar_tensor_tensor(out=logit[:, :, 0], in0=cback, scalar=cin[:, bass.DynSlice(n, 1)],
                                       in1=logit[:, :, 0], op0=ALU.add, op1=ALU.max).then_inc(s("carry_b"), 1)
                after(dve, s("carry_b"), n)
                v.tensor_tensor_scan(pre2[:, :, :].rearrange(flat), cont4[:, :, :].rearrange(flat),
                                     logit[:, :, :].rearrange(flat), -BIG, ALU.add, ALU.max)\
                    .then_inc(s("pre2_b"), 1)
                last = isl[:, bass.DynSlice(n, 1), :].rearrange("p a (j c) -> p (a j) c", c=1)
                v.tensor_copy(peaks[:, :, H:H + 1], last).then_inc(s("pkl_b"), 1)
                after(dve, s("pre2_b"), n)
                v.tensor_tensor(peaks[:, :, 0:H], pre2[:, :, :].rearrange("p h j -> p j h"),
                                last.to_broadcast([128, J, H]), ALU.mult).then_inc(s("pk_b"), 1)
                after(dve, s("mg_b"), n)
                v.tensor_scalar(pen[:, :], mg[:, H:H + 1], -1.0, BIG, ALU.add, ALU.mult).then_inc(s("pen_b"), 1)
                dve.wait_ge(s("st_load"), n * 32 + 32)
                after(dve, s("pen_b"), n)
                v.scalar_tensor_tensor(out=newold[b][:, 0, :], in0=mg[:, 0:H], scalar=pen[:, 0:1],
                                       in1=newold[b][:, 1, :], op0=ALU.add, op1=ALU.max)\
                    .then_inc(s("mnew_b"), 1)
                after(dve, s("mnew_b"), n)
                v.tensor_tensor(nu[:, :].rearrange("p (a h) -> p a h", h=H), newold[b][:, :, :],
                                node[b][:, 0:H].rearrange("p (a h) -> p a h", a=1).to_broadcast([128, 2, H]),
                                ALU.add).then_inc(s("nu_b"), 1)
                after(dve, s("nu_b"), n)
                v.scalar_tensor_tensor(out=node[b][:, H:3 * H], in0=nu[:, :], scalar=SLOPE, in1=nu[:, :],
                                       op0=ALU.mult, op1=ALU.max).then_inc(s("node_b"), 1)
                after(dve, s("node_b"), n)
                v.tensor_tensor(fd[:, :], node[b][:, 2 * H:3 * H], node[b][:, H:2 * H], ALU.subtract)\
                    .then_inc(s("fd_b"), 1)
                after(dve, s("look"), n)
                v.tensor_tensor(lin[:, :, :], V[b][:, :, C:C + H], lk[:, :, 0:H], ALU.add).then_inc(s("lin_b"), 1)
                after(dve, s("lin_b"), n)
                v.scalar_tensor_tensor(out=lre[:, :, :], in0=lin[:, :, :], scalar=SLOPE, in1=lin[:, :, :],
                                       op0=ALU.mult, op1=ALU.max).then_inc(s("lre_b"), 1)
                after(dve, s("lre_b"), n)
                v.tensor_tensor(lin[:, :, :], lre[:, :, :], lk[:, :, H:2 * H], ALU.subtract)\
                    .then_inc(s("zs_b"), 1)
                after(dve, s("zs_b"), n)
                v.tensor_scalar(lre[:, :, :], lin[:, :, :], 0.0, None, ALU.min).then_inc(s("zm_b"), 1)
                after(dve, s("wp_b"), n)
                v4 = V[b][:, :, 0:C].rearrange("p j (h f) -> p j h f", f=F)
                v.tensor_tensor(v4, v4, wps.rearrange("p j (h a) -> p j h a", a=1)
                                .to_broadcast([128, J, H, F]), ALU.mult).then_inc(s("vw_b"), 1)
            pairs(dve, item, 0, NG // 2)
            merge(NG - 1, 1)

            dve.wait_ge(s("sum_in"), 32)
            dn = allsum[0:NP, :, C:C + H]
            link(v.reciprocal(rden[0:NP, :, :], dn))
            for h in range(H):
                part = allsum[0:NP, :, h * F:(h + 1) * F]
                link(v.tensor_tensor(part, part, rden[0:NP, :, h:h + 1].to_broadcast([NP, NT, F]), ALU.mult))
            full = allsum[0:NP, :, 0:C]
            link(v.tensor_tensor(full, full, b0s[0:NP, :].rearrange("p (a c) -> p a c", a=1)
                                 .to_broadcast([NP, NT, C]), ALU.add))
            link(v.scalar_tensor_tensor(out=xs[0:NP, :, :], in0=full, scalar=0.0, in1=xs[0:NP, :, :],
                                        op0=ALU.max, op1=ALU.add))
            layernorm(2, NT)

            def node1(t, b, it):
                n = t + NT
                dve.wait_ge(s("h_tr"), n + 1)
                dve.wait_ge(s("h_mm"), n - 1)
                v.tensor_copy(hT[b][:, :, 0:NP], pt[b][:, 0:256].rearrange("p (a c) -> p a c", a=2)[:, :, 0:NP])\
                    .then_inc(s("h_trc"), 1)
                dve.wait_ge(s("h_mm"), n + 1)
                v.scalar_tensor_tensor(out=row(tab, t, 0, C), in0=bew[0:NP, :],
                                       scalar=row(allsum, t, TAB - 1, TAB), in1=pv[b][0:NP, 0:C],
                                       op0=ALU.mult, op1=ALU.add).then_inc(s("h_ev"), 1)
            pairs(dve, node1, 0, NT // 2)
            dve.wait_ge(s("h_ev"), 2 * NT)
            v.tensor_copy(pen[:, :], b1s[:, :]).then_inc(s("tab1_done"), 1)
            v.tensor_tensor(xs[0:NP, :, :], xs[0:NP, :, :], b2s[0:NP, :].rearrange("p (a c) -> p a c", a=1)
                            .to_broadcast([NP, NT, C]), ALU.add).then_inc(s("b2add"), 1)

            def item2(n, b, it):
                after(dve, s("vm2"), n, 2)
                select(n, b, "sel2")
                dve.wait_ge(s("z_load"), n * 16 + 16)
                after(dve, s("vm2"), n)
                v.tensor_tensor(state[:, 0:C], state[:, 0:C], pv[b][:, 0:C], ALU.add).then_inc(s("z_add"), 1)
            pairs(dve, item2, 0, NG // 2)

            dve.wait_ge(s("b2add"), 1)

            def node2(t, b, it):
                after(dve, s("zc_m"), t)
                v.tensor_tensor(row(tab, t, 0, C), pv[b][0:NP, 0:C], row(xs, t, 0, C), ALU.add)\
                    .then_inc(s("zc_o"), 1)
            pairs(dve, node2, 0, NT // 2)


CONSTS = 1 + 2 * H + 4 + 2 + 2
PADS = 0
for _wd in (H, H, ST, C):
    PADS += -(-((NPAD - N) // 75 * _wd) // (ST - C - H))

_INS = ['x', 'src', 'dst', 'edge_attr_128', 'L0_gnn_W', 'L0_gnn_att_src', 'L0_gnn_att_dst', 'L0_gnn_bias',
        'L1_gnn_We', 'L1_gnn_be', 'L1_gnn_W1', 'L1_gnn_b1', 'L1_gnn_W2', 'L1_gnn_b2']


def kernel(**inputs):
    import numpy as _np
    import concourse.bacc as _bacc
    from concourse import mybir as _mybir
    from concourse.bass_utils import run_bass_kernel_spmd as _run

    nc = _bacc.Bacc("TRN2", target_bir_lowering=False, num_devices=1)
    arrays, args = {}, []
    for name in _INS:
        a = _np.ascontiguousarray(inputs[name])
        arrays[f"in_{name}_dram"] = a
        args.append(nc.dram_tensor(f"in_{name}_dram", a.shape, _mybir.dt.from_np(a.dtype), kind="ExternalInput").ap())
    args.append(nc.dram_tensor("out_0_dram", (N, C), _mybir.dt.float32, kind="ExternalOutput").ap())
    gnn_kernel(nc, *args)
    r = _run(nc, [arrays], core_ids=[0])
    return r.results[0]["out_0_dram"]
```

```python
import concourse.bass as bass
from concourse import mybir
from contextlib import ExitStack

FP32 = mybir.dt.float32
INT32 = mybir.dt.int32
BF16 = mybir.dt.bfloat16
ALU = mybir.AluOpType
ACT = mybir.ActivationFunctionType
AX = mybir.AxisListType

N = 6250
E = 200000
C = 128
H = 4
F = C // H
SLOPE = 0.2
EPS = 1e-5

NP = 125
NT = N // NP
SPLIT = 112

J = 16
GE = 128 * J
NG = -(-E // GE)
LAST = E - GE
DUP = (NG * GE - E) // J
assert DUP * J == NG * GE - E and NG % 2 == 0 and NP * NT == N
WIN = 128
NPAD = N + 150
BIG = 1e30
FAR = 1e6

NX = 48
assert NX >= N // WIN and NX % 2 == 0
DUMMY = N

TAB = C + H + 1
TW = TAB + H
NK = 3
DL = H + NK * H // 2
QUART = J // 4
ST = TAB + C


def gnn_kernel(nc, x, src, dst, attr, W, att_src, att_dst, bias0, We, be, W1, b1, W2, b2, out):
    ctx = ExitStack()
    with ctx:
        def sb(name, shape, dt=FP32):
            return ctx.enter_context(nc.sbuf_tensor(name, shape, dt))

        def sem(name):
            return ctx.enter_context(nc.semaphore(name))

        def dram(name, shape):
            return nc.dram_tensor(name, shape, FP32, kind="Internal").ap()

        table0 = dram("table0", [N, TAB])
        table1 = dram("table1", [N, C])
        dlogit = dram("dlogit", [NPAD, DL])
        peak = dram("peak", [NPAD, H])
        sums0 = dram("sums0", [NPAD, ST])
        sums1 = dram("sums1", [NPAD, C])

        xs = sb("xs", [128, NT, C])
        tab = sb("tab", [128, NT, TW])
        big = sb("big", [128, NT * ST])
        V = [big[:, b * J * TAB:(b + 1) * J * TAB].rearrange("p (j c) -> p j c", c=TAB) for b in range(2)]
        o = 2 * J * TAB
        AT = [big[:, o + b * J * C:o + (b + 1) * J * C].rearrange("p (j c) -> p j c", c=C) for b in range(2)]
        o += 2 * J * C
        SEL = [big[:, o + b * J * WIN:o + (b + 1) * J * WIN].rearrange("p (j w) -> p j w", w=WIN)
               for b in range(2)]
        assert o + 2 * J * WIN <= NT * ST
        allsum = big[:, :].rearrange("p (t c) -> p t c", c=ST)
        zin = big[:, 0:NT * C].rearrange("p (t c) -> p t c", c=C)
        selH = sb("selH", [128, J, WIN], BF16)
        selT = sb("selT", [128, J * 128], BF16)
        identH = sb("identH", [128, 128], BF16)
        dlog = sb("dlog", [128, NT, DL])
        dres = sb("dres", [128, NT, H])
        dsti = sb("dsti", [128, NG, J], INT32)
        dd = sb("dd", [128, NG, J])
        drel = sb("drel", [128, NG, J])
        cont = sb("cont", [128, NG, J])
        isl = sb("isl", [128, NG, J])
        cin = sb("cin", [128, NG])
        thru = sb("thru", [128, NG])
        firsts = sb("firsts", [128, NG])
        lasts = sb("lasts", [128, NG])
        basei = sb("basei", [1, NG], INT32)
        idx = [sb(f"idx{b}", [128, J], INT32) for b in range(2)]
        iotaf = sb("iotaf", [128, 128])
        ident = sb("ident", [128, 128])
        shp = sb("shp", [128, 128])
        shn = sb("shn", [128, 128])
        pick = [sb(f"pick{i}", [128, 128]) for i in range(3)]
        edgefix = sb("edgefix", [128, 2])
        wcat = sb("wcat", [128, TW])
        wT = sb("wT", [128, 128])
        weT = sb("weT", [128, 128])
        attm = sb("attm", [128, 2 * H + 1])
        wes = sb("wes", [128, C])
        w1a = sb("w1a", [128, C])
        w1b = sb("w1b", [128, C])
        wew = sb("wew", [128, C])
        w2s = sb("w2s", [128, C])
        bes = sb("bes", [128, 1])
        beb = sb("beb", [128, 128])
        bew = sb("bew", [128, C])
        b0s = sb("b0s", [128, C])
        b2s = sb("b2s", [128, C])
        b1s = sb("b1s", [128, 1])
        init = sb("init", [128, ST - C])
        stat = sb("stat", [128, NT, 6])
        lnw = sb("lnw", [128, 4, NT])
        rstd = sb("rstd", [128, NT])
        nmr = sb("nmr", [128, NT])
        epsc = sb("epsc", [128, 1])
        rden = sb("rden", [128, NT, H])
        hb = [sb(f"hb{b}", [128, 2, 128]) for b in range(2)]
        hT = [sb(f"hT{b}", [128, 2, 128]) for b in range(2)]
        cont4 = sb("cont4", [128, H, J])
        logit = sb("logit", [128, H, J])
        pre1 = sb("pre1", [128, H, J])
        pre2 = sb("pre2", [128, H, J])
        thru4 = [sb(f"thru4{b}", [128, H]) for b in range(2)]
        thruT = sb("thruT", [H, 128])
        tails = sb("tails", [H, 129])
        pkf = sb("pkf", [128, J, H])
        pkr = sb("pkr", [128, J, H])
        peaks = sb("peaks", [128, J, NK * H + 1], BF16)
        mgs = sb("mgs", [128, H])
        shr = sb("shr", [128, H])
        lks = sb("lks", [128, J, 2 * H])
        pen = sb("pen", [128, 1])
        newold = [sb(f"newold{b}", [128, 2, H]) for b in range(2)]
        node = [sb(f"node{b}", [128, DL + NK * H // 2 + 2 * H]) for b in range(2)]
        SH = DL + NK * H // 2
        parts = [node[b][:, H:SH].bitcast(BF16) for b in range(2)]
        fold = [sb(f"fold{b}", [128, H]) for b in range(2)]
        lin = sb("lin", [128, J, H])
        lre = sb("lre", [128, J, H])
        state = sb("state", [128, ST])
        nu = sb("nu", [128, 2 * H])
        fd = sb("fd", [128, H])

        def bank(name):
            return ctx.enter_context(nc.psum_tensor(name, [128, 512], FP32))
        pv = [bank(f"pv{b}") for b in range(2)]
        pa = [bank(f"pa{b}") for b in range(2)]
        pt = [bank(f"pt{b}") for b in range(2)]
        pc = bank("pc")
        pm = bank("pm")
        iotap = pc[:, 0:128]
        tailT = pm[0:H, 0:128]
        thruP = pm[0:H, 128:256]
        cback = pm[:, 256:256 + H]
        mg = pm[:, 264:264 + NK * H + 1]
        lk = pv[1][:, 0:2 * NK * H * J].rearrange("p (j c) -> p j c", c=2 * NK * H)
        ptH = [pt[b][:, :].bitcast(BF16) for b in range(2)]
        wps = pm[:, 400:400 + H * J].rearrange("p (j c) -> p j c", c=H)

        S = {}

        def s(name):
            if name not in S:
                S[name] = sem(name)
            return S[name]

        names = """x_in idx_dst consts_in ones_done ident_done iota_p
            pool_c w_t w_tc w_aux w_auxc prep d_f shifted masks drel_done base_i
            stats ln_a ln_sq ln_b h_ready h_tr h_trc h_mm h_ev tab_done pad_z tab_out pad_out
            idx0 idx1 gat0 gat1 attr0 attr1 g_started
            st_load m_store s_load s_store
            sel_b cont_b log_b pre1_b tailT_b thruT_b tails_b cback_b carry_b pre2_b pk_b pkl_b mg_b pen_b
            mnew_b nu_b node_b fd_b fold_b sttr stcp look lin_b lre_b zs_b zm_b w_b wp_b vw_b am_b vm_b
            ms_b mt_b mu_b merged
            sum_in den_r o_n o_b o_r x1_done ln2 y_ready tab1_done tab1_out zpad
            thru_c selh_b pkf_b pr_b pk1_b pk2_b mgs_b sh0_b sr_b sh1_b sh2_b lks_b dl thru4_b chain beb_done i20 i21 g20 g21 sel2 vm2 z_load z_add z_store g2_started
            z_in zc_r zc_t zc_u zc_m zc_o out_w b2add""".split()
        for n_ in names:
            s(n_)

        block = ctx.enter_context(nc.Block())

        def nodes(ap, width_from, width_to):
            return ap[0:N, width_from:width_to].rearrange("(p t) c -> p t c", t=NT)

        def after(eng, sm, n, lag=0):
            if isinstance(n, int) and n - lag < 0:
                return
            eng.wait_ge(sm, n + (1 - lag))

        def after_dma(eng, sm, count):
            if isinstance(count, int) and count <= 0:
                return
            eng.wait_ge(sm, count * 16)

        def pairs(eng, body, first, count, peel_last=False):
            lo = first
            if first == 0:
                for b in range(2):
                    body(b, b, 0)
                lo = 1
            hi = first + count - (1 if peel_last else 0)
            with eng.Fori(lo, hi) as it:
                for b in range(2):
                    body(it * 2 + b, b, it)
            if peel_last:
                for b in range(2):
                    body(2 * hi + b, b, hi)

        @block.sync
        def _(sp):
            for lo, hi in ((0, SPLIT), (SPLIT, NP)):
                sp.dma_start(xs[lo:hi, :, :], nodes(x, 0, C)[lo:hi]).then_inc(s("x_in"), 16)
            sp.wait_ge(s("prep"), 1)
            sp.dma_start(wcat[:, 0:C], W).then_inc(s("consts_in"), 16)
            for h in range(H):
                sp.dma_start(attm[h * F:(h + 1) * F, h:h + 1],
                             att_src[h, :].rearrange("(f a) -> f a", a=1)).then_inc(s("consts_in"), 16)
                sp.dma_start(attm[h * F:(h + 1) * F, H + 1 + h:H + 2 + h],
                             att_dst[h, :].rearrange("(f a) -> f a", a=1)).then_inc(s("consts_in"), 16)
            sp.dma_start(wes[:, :], We).then_inc(s("consts_in"), 16)
            sp.dma_start(w1a[:, :], W1[0:C, :]).then_inc(s("consts_in"), 16)
            sp.dma_start(w1b[:, :], W1[C:2 * C, :]).then_inc(s("consts_in"), 16)
            sp.dma_start(w2s[:, :], W2).then_inc(s("consts_in"), 16)
            sp.dma_start(bes[:, :], be.rearrange("(p a) -> p a", a=1)).then_inc(s("consts_in"), 16)
            sp.dma_start(b1s[:, :], b1.rearrange("(p a) -> p a", a=1)).then_inc(s("consts_in"), 16)
            sp.dma_start(b0s[:, :], bias0.rearrange("(a n) -> a n", a=1).to_broadcast([128, C]))\
                .then_inc(s("consts_in"), 16)
            sp.dma_start(b2s[:, :], b2.rearrange("(a n) -> a n", a=1).to_broadcast([128, C]))\
                .then_inc(s("consts_in"), 16)
            sp.dma_start(dsti[:, 0:NG - 1, :],
                         dst[0:(NG - 1) * GE].rearrange("(g p j) -> p g j", p=128, j=J))\
                .then_inc(s("idx_dst"), 16)
            sp.dma_start(dsti[:, NG - 1, :], dst[LAST:E].rearrange("(p j) -> p j", j=J))\
                .then_inc(s("idx_dst"), 16)

            sp.wait_ge(s("pad_z"), 1)
            pads = NPAD - N
            zero = init[:, H:H + 1]
            for ap, wd in ((dlogit, DL), (peak, H), (sums0, ST), (sums1, C)):
                rows = ap[N:NPAD, :].rearrange("(p q) c -> p (q c)", p=75)
                n_el = pads // 75 * wd
                done = 0
                while done < n_el:
                    k = min(n_el - done, ST - C - H)
                    sp.dma_start(rows[:, done:done + k], init[0:75, H:H + k]).then_inc(s("pad_out"), 16)
                    done += k

            sp.wait_ge(s("tab_done"), 1)
            for lo, hi in ((0, SPLIT), (SPLIT, NP)):
                sp.dma_start(nodes(dlogit, 0, DL)[lo:hi], dlog[lo:hi, :, :]).then_inc(s("tab_out"), 16)
                for ap, to, frm, wd in ((table0, 0, 0, TAB), (peak, 0, C, H), (sums0, 0, 0, C)):
                    sp.dma_start(nodes(ap, to, to + wd)[lo:hi], tab[lo:hi, :, frm:frm + wd])\
                        .then_inc(s("tab_out"), 16)
                sp.dma_start(nodes(sums0, C, ST)[lo:hi],
                             init[lo:hi, :].rearrange("p (a c) -> p a c", a=1).to_broadcast([hi - lo, NT, ST - C]))\
                    .then_inc(s("tab_out"), 16)

            def load_edges(n, b, it, start):
                after_dma(sp, s(f"gat{b}"), it * J)
                sp.dma_start(idx[b][:, :], src[bass.DynSlice(start, GE)].rearrange("(p j) -> p j", j=J))\
                    .then_inc(s(f"idx{b}"), 16)
                after(sp, s("am_b"), n, 2)
                sp.dma_start(AT[b], attr[bass.DynSlice(start, GE), :].rearrange("(p j) c -> p j c", j=J))\
                    .then_inc(s(f"attr{b}"), 16)

            def load_peak(n, b, base):
                after_dma(sp, s("m_store"), n)
                sp.dma_start(newold[b][:, 1, :], peak[bass.DynSlice(base, WIN), :]).then_inc(s("st_load"), 16)
                sp.dma_start(node[b][:, 0:DL], dlogit[bass.DynSlice(base, WIN), :]).then_inc(s("st_load"), 16)

            def store_peak(n, b, base):
                after(sp, s("mnew_b"), n)
                sp.dma_start(peak[bass.DynSlice(base, WIN), :], newold[b][:, 0, :]).then_inc(s("m_store"), 16)

            def update_sums(n, base):
                after_dma(sp, s("s_store"), n)
                sp.dma_start(state[:, :], sums0[bass.DynSlice(base, WIN), :]).then_inc(s("s_load"), 16)
                after(sp, s("merged"), n)
                sp.dma_start(sums0[bass.DynSlice(base, WIN), :], state[:, :]).then_inc(s("s_store"), 16)

            sp.wait_ge(s("base_i"), 1)
            sp.wait_ge(s("pad_out"), 16 * PADS)
            sp.wait_ge(s("tab_out"), 16 * 10)

            def base_of(g):
                return sp.value_load(basei[0:1, bass.DynSlice(g, 1)], min_val=0, max_val=N)

            def item(n, b, it):
                if isinstance(n, int) and n < 2:
                    load_edges(n, b, it, n * GE)
                base = base_of(n)
                load_peak(n, b, base)
                if not (isinstance(n, int) and n == 0):
                    update_sums(n - 1, base_of(n - 1))
                store_peak(n, b, base)
                if isinstance(n, int) and n + 2 >= NG - 1:
                    if n + 2 == NG - 1:
                        load_edges(n + 2, b, it + 1, LAST)
                elif isinstance(n, int) and n + 2 >= NG:
                    pass
                else:
                    load_edges(n + 2, b, it + 1, (n + 2) * GE)

            for b in range(2):
                item(b, b, 0)
            with sp.Fori(1, NG // 2 - 2) as it:
                for b in range(2):
                    item(it * 2 + b, b, it)
            for it in range(NG // 2 - 2, NG // 2):
                for b in range(2):
                    item(it * 2 + b, b, it)
            update_sums(NG - 1, base_of(NG - 1))

            sp.wait_ge(s("s_store"), 16 * NG)
            for lo, hi in ((0, SPLIT), (SPLIT, NP)):
                sp.dma_start(allsum[lo:hi], nodes(sums0, 0, ST)[lo:hi]).then_inc(s("sum_in"), 16)
            sp.wait_ge(s("tab1_done"), 1)
            for lo, hi in ((0, SPLIT), (SPLIT, NP)):
                sp.dma_start(nodes(table1, 0, C)[lo:hi], tab[lo:hi, :, 0:C]).then_inc(s("tab1_out"), 16)
                sp.dma_start(nodes(sums1, 0, C)[lo:hi], tab[lo:hi, :, 0:C]).then_inc(s("tab1_out"), 16)

            def load_idx(n, b, it, start):
                after_dma(sp, s(f"g2{b}"), it * J)
                sp.dma_start(idx[b][:, :], src[bass.DynSlice(start, GE)].rearrange("(p j) -> p j", j=J))\
                    .then_inc(s(f"i2{b}"), 16)

            def update_z(n, base):
                after_dma(sp, s("z_store"), n)
                sp.dma_start(state[:, 0:C], sums1[bass.DynSlice(base, WIN), :]).then_inc(s("z_load"), 16)
                after(sp, s("z_add"), n)
                sp.dma_start(sums1[bass.DynSlice(base, WIN), :], state[:, 0:C]).then_inc(s("z_store"), 16)

            sp.wait_ge(s("tab1_out"), 16 * 4)
            for b in range(2):
                load_idx(b, b, 0, b * GE)

            def item2(n, b, it):
                if isinstance(n, int) and n + 2 >= NG - 1:
                    if n + 2 == NG - 1:
                        load_idx(n + 2, b, it + 1, LAST)
                elif not (isinstance(n, int) and n + 2 >= NG):
                    load_idx(n + 2, b, it + 1, (n + 2) * GE)
                update_z(n, base_of(n))

            for b in range(2):
                item2(b, b, 0)
            with sp.Fori(1, NG // 2 - 2) as it:
                for b in range(2):
                    item2(it * 2 + b, b, it)
            for it in range(NG // 2 - 2, NG // 2):
                for b in range(2):
                    item2(it * 2 + b, b, it)
            sp.wait_ge(s("z_store"), 16 * NG)
            for lo, hi in ((0, SPLIT), (SPLIT, NP)):
                sp.dma_start(zin[lo:hi], nodes(sums1, 0, C)[lo:hi]).then_inc(s("z_in"), 16)
            sp.wait_ge(s("zc_o"), NT)
            for lo, hi in ((0, SPLIT), (SPLIT, NP)):
                sp.dma_start(nodes(out, 0, C)[lo:hi], tab[lo:hi, :, 0:C]).then_inc(s("out_w"), 16)
            sp.wait_ge(s("out_w"), 32)

        @block.gpsimd
        def _(pool):
            pool.memset(attm[:, :], 0.0).then_inc(s("prep"), 1)
            pool.memset(wcat[:, C:TW], 0.0).then_inc(s("pool_c"), 1)
            pool.memset(init[:, 0:H], 1.0).then_inc(s("pool_c"), 1)
            pool.memset(init[:, H:ST - C], 0.0).then_inc(s("pool_c"), 1)
            pool.wait_ge(s("pool_c"), 3)
            pool.iota(iotaf[:, :], [[1, 128]], base=0, channel_multiplier=0,
                      allow_small_or_imprecise_dtypes=True).then_inc(s("pad_z"), 1)
            tiles = [(ident, 0, 1, [[-1, 128]]), (shp, 1, 1, [[-1, 128]]), (shn, -1, 1, [[-1, 128]]),
                     (pick[0], 0, 1, [[0, 128]]), (pick[1], -127, 1, [[0, 128]]), (pick[2], -DUP, 1, [[0, 128]])]
            for tl, _, _, _ in tiles:
                pool.memset(tl[:, :], 0.0).then_inc(s("pool_c"), 1)
            pool.memset(edgefix[:, :], 0.0).then_inc(s("pool_c"), 1)
            pool.memset(epsc[:, :], EPS).then_inc(s("pool_c"), 1)
            pool.memset(tails[:, :], -BIG).then_inc(s("pool_c"), 1)
            pool.wait_ge(s("pool_c"), 12)
            for tl, base, cm, pat in tiles:
                pool.affine_select(out=tl[:, :], in_=tl[:, :], compare_op=ALU.not_equal, fill=1.0,
                                   base=base, pattern=pat, channel_multiplier=cm).then_inc(s("pool_c"), 1)
            for c, base in ((0, 0), (1, -127)):
                pool.affine_select(out=edgefix[:, c:c + 1], in_=edgefix[:, c:c + 1], compare_op=ALU.not_equal,
                                   fill=-1.0, base=base, pattern=[[0, 1]], channel_multiplier=1)\
                    .then_inc(s("pool_c"), 1)

            def gather(b, it, rows, table, gat, ix, started, n=None):
                pool.wait_ge(s(f"{ix}{b}"), it * 16 + 16)
                pool.sem_inc(s(started), 1)
                for j in range(J):
                    if n is not None and j % QUART == 0 and not (isinstance(n, int) and n < 2):
                        pool.wait_ge(s("vm_b"), n * 4 + (j // QUART - 7))
                        pool.sem_inc(s(started), 1)
                    pool.indirect_dma_start(
                        out=V[b][:, j, 0:rows], out_offset=None, in_=table,
                        in_offset=bass.IndirectOffsetOnAxis(ap=idx[b][:, j:j + 1], axis=0))\
                        .then_inc(s(f"{gat}{b}"), 16)

            pool.wait_ge(s("tab_out"), 16 * 10)

            def item(n, b, it):
                gather(b, it, TAB, table0, "gat", "idx", "g_started", n)
            pairs(pool, item, 0, NG // 2)

            pool.wait_ge(s("tab1_out"), 16 * 4)

            def item2(n, b, it):
                after(pool, s("vm2"), n, 2)
                gather(b, it, C, table1, "g2", "i2", "g2_started")
            pairs(pool, item2, 0, NG // 2)

        @block.scalar
        def _(act):
            def a(out_, in_, func, name, **kw):
                return nc.scalar.activation(out_, in_, func, **kw).then_inc(s(name), 1)

            act.wait_ge(s("pad_z"), 1)
            a(iotap, iotaf[:, :], ACT.Copy, "iota_p")
            act.wait_ge(s("pool_c"), 20)
            a(identH[:, :], ident[:, :], ACT.Copy, "iota_p")
            act.wait_ge(s("w_t"), 2)
            a(wT[:, :], pt[0][:, 0:128], ACT.Copy, "w_tc")
            a(weT[:, :], pt[0][:, 128:256], ACT.Copy, "w_tc")
            act.wait_ge(s("w_aux"), 3)
            a(wcat[:, C:TW], pt[1][:, 0:2 * H + 1], ACT.Copy, "w_auxc")
            a(wew[:, :], pt[1][:, 128:256], ACT.Copy, "w_auxc")
            a(bew[:, :], pt[1][:, 256:384], ACT.Copy, "w_auxc")

            def standard_deviation(k):
                act.wait_ge(s("ln_a"), k)
                a(lnw[0:NP, 1, :], lnw[0:NP, 0, :], ACT.Sqrt, "ln_sq", bias=epsc[0:NP, 0:1])

            def normalised(t, b, k, lag_name):
                a(hb[b][0:NP, 0, :], xs[0:NP, bass.DynSlice(t, 1), :].rearrange("p a c -> p (a c)"),
                  ACT.Relu, "h_ready", scale=rstd[0:NP, bass.DynSlice(t, 1)],
                  bias=nmr[0:NP, bass.DynSlice(t, 1)])

            standard_deviation(1)
            act.wait_ge(s("ln_b"), 1)

            def node0(t, b, it):
                after(act, s("h_tr"), t, 2)
                normalised(t, b, 0, None)
            pairs(act, node0, 0, NT // 2)

            def item(n, b, it):
                after(act, s("sel_b"), n)
                after(act, s("mg_b"), n, 1)
                a(selH[:, :, :], SEL[b], ACT.Copy, "selh_b")
                after(act, s("thruT_b"), n)
                if not (isinstance(n, int) and n == 0):
                    act.wait_ge(s("tails_b"), n)
                a(thruT[:, :], thruP, ACT.Copy, "thru_c")
                after(act, s("look"), n, 1)
                for r in range(2):
                    act.wait_ge(s("sttr"), n * 2 + (r + 1))
                    a(selT[:, r * 1024:(r + 1) * 1024], ptH[r], ACT.Copy, "stcp")
                after(act, s("fd_b"), n)
                a(fold[b][:, :], fd[:, :], ACT.Exp, "fold_b")
                after(act, s("zm_b"), n)
                a(wps, lre[:, :, :], ACT.Exp, "wp_b")
                a(V[b][:, :, C:C + H], lre[:, :, :], ACT.Exp, "w_b")
            pairs(act, item, 0, NG // 2)

            standard_deviation(2)
            act.wait_ge(s("ln_b"), 2)

            def node1(t, b, it):
                n = t + NT
                act.wait_ge(s("h_tr"), n - 1)
                normalised(t, b, 1, None)
                a(hb[b][0:NP, 1, :], allsum[0:NP, bass.DynSlice(t, 1), TAB:ST].rearrange("p a c -> p (a c)"),
                  ACT.Copy, "y_ready")
            pairs(act, node1, 0, NT // 2)

            act.wait_ge(s("z_in"), 32)

            def node2(t, b, it):
                after(act, s("zc_t"), t, 2)
                a(hb[b][0:NP, 0, :], zin[0:NP, bass.DynSlice(t, 1), :].rearrange("p a c -> p (a c)"),
                  ACT.Copy, "zc_r")
                after(act, s("zc_t"), t)
                a(hT[b][:, 0, 0:NP], pt[b][:, 0:NP], ACT.Relu, "zc_u", bias=b1s[:, 0:1])
            pairs(act, node2, 0, NT // 2)

        @block.tensor
        def _(pe):
            pe.wait_ge(s("pool_c"), 20)
            pe.wait_ge(s("consts_in"), 16 * CONSTS)
            nc.tensor.transpose(pt[0][:, 0:128], wcat[:, 0:C], ident[:, :]).then_inc(s("w_t"), 1)
            nc.tensor.transpose(pt[0][:, 128:256], wes[:, :], ident[:, :]).then_inc(s("w_t"), 1)
            pe.wait_ge(s("w_tc"), 2)
            nc.tensor.matmul(pt[1][:, 0:2 * H + 1], wT[:, :], attm[:, :], start=True, stop=True)\
                .then_inc(s("w_aux"), 1)
            nc.tensor.matmul(pt[1][:, 128:256], weT[:, :], w1b[:, :], start=True, stop=True)\
                .then_inc(s("w_aux"), 1)
            pe.wait_ge(s("beb_done"), 1)
            nc.tensor.matmul(pt[1][:, 256:384], beb[:, :], w1b[:, :], start=True, stop=True)\
                .then_inc(s("w_aux"), 1)
            pe.wait_ge(s("d_f"), 2)
            nc.tensor.matmul(pa[0][:, 0:NG], shp[:, :], dd[:, :, J - 1], start=True, stop=True)\
                .then_inc(s("shifted"), 1)
            nc.tensor.matmul(pa[0][:, 128:128 + NG], shn[:, :], dd[:, :, 0], start=True, stop=True)\
                .then_inc(s("shifted"), 1)
            nc.tensor.matmul(pa[0][:, 256:256 + NG - 1], pick[0][:, :], dd[:, 0:NG - 1, 0], start=True, stop=True)\
                .then_inc(s("shifted"), 1)
            nc.tensor.matmul(pa[0][:, 256 + NG - 1:256 + NG], pick[2][:, :], dd[:, NG - 1, 0:1],
                             start=True, stop=True).then_inc(s("shifted"), 1)
            nc.tensor.matmul(pa[0][:, 384:384 + NG], pick[1][:, :], dd[:, :, J - 1], start=True, stop=True)\
                .then_inc(s("shifted"), 1)

            pe.wait_ge(s("w_auxc"), 3)

            def node0(t, b, it):
                after(pe, s("h_ready"), t)
                after(pe, s("h_trc"), t, 2)
                nc.tensor.transpose(pt[b][:, 0:NP], hb[b][0:NP, 0, :], ident[0:NP, 0:NP]).then_inc(s("h_tr"), 1)
                after(pe, s("h_trc"), t)
                after(pe, s("h_ev"), t, 2)
                nc.tensor.matmul(pv[b][0:NP, 0:TW], hT[b][:, 0, 0:NP], wcat[:, :], start=True, stop=True)\
                    .then_inc(s("h_mm"), 1)
            pairs(pe, node0, 0, NT // 2)

            def item(n, b, it):
                def attribute_sums(lo, hi):
                    for j in range(lo, hi):
                        ins = nc.tensor.matmul(pa[b][:, 0:C], SEL[b][:, j, :], AT[b][:, j, :],
                                               start=(j == 0), stop=(j == J - 1))
                    return ins

                after(pe, s("thru4_b"), n)
                nc.tensor.transpose(thruP, thru4[b][:, :], ident[:, :]).then_inc(s("thruT_b"), 1)
                after(pe, s("selh_b"), n)
                for r in range(2):
                    if not (isinstance(n, int) and n == 0):
                        pe.wait_ge(s("stcp"), n * 2 + (r - 1))
                    for q in range(8):
                        ins = nc.tensor.transpose(ptH[r][:, q * 128:(q + 1) * 128],
                                                  selH[:, 8 * r + q, :], identH[:, :])
                    ins.then_inc(s("sttr"), 1)
                after(pe, s("pre1_b"), n)
                after(pe, s("thru_c"), n)
                nc.tensor.transpose(tailT, pre1[:, :, J - 1], ident[:, :]).then_inc(s("tailT_b"), 1)
                after(pe, s("tails_b"), n)
                nc.tensor.matmul(cback, tails[:, 0:128], ident[0:H, 0:H], start=True, stop=True)\
                    .then_inc(s("cback_b"), 1)
                pe.wait_ge(s(f"attr{b}"), it * 16 + 16)
                after(pe, s("merged"), n, 2)
                attribute_sums(0, J // 2)
                after(pe, s("pkl_b"), n)
                after(pe, s("pk2_b"), n)
                for j in range(J):
                    ins = nc.tensor.matmul(mg, selH[:, j, :], peaks[:, j, :], start=(j == 0), stop=(j == J - 1))
                ins.then_inc(s("mg_b"), 1)
                attribute_sums(J // 2, J).then_inc(s("am_b"), 1)
                after(pe, s("sh2_b"), n)
                pe.wait_ge(s("stcp"), n * 2 + 2)
                for j in range(J):
                    ins = nc.tensor.matmul(lk[:, j, :], selT[:, j * 128:(j + 1) * 128], parts[b],
                                           start=True, stop=True)
                ins.then_inc(s("look"), 1)
                after(pe, s("w_b"), n)
                for q in range(4):
                    pe.wait_ge(s("vw_b"), n * 4 + (q + 1))
                    for j in range(q * QUART, (q + 1) * QUART):
                        ins = nc.tensor.matmul(pv[0][:, 0:TAB], SEL[b][:, j, :], V[b][:, j, :],
                                               start=(j == 0), stop=(j == J - 1))
                    ins.then_inc(s("vm_b"), 1)
            pairs(pe, item, 0, NG // 2)

            def node1(t, b, it):
                after(pe, s("y_ready"), t)
                n = t + NT
                pe.wait_ge(s("h_ready"), n + 1)
                pe.wait_ge(s("h_trc"), n - 1)
                nc.tensor.transpose(pt[b][:, 0:NP], hb[b][0:NP, 0, :], ident[0:NP, 0:NP])
                nc.tensor.transpose(pt[b][:, 128:128 + NP], hb[b][0:NP, 1, :], ident[0:NP, 0:NP])\
                    .then_inc(s("h_tr"), 1)
                pe.wait_ge(s("h_trc"), n + 1)
                pe.wait_ge(s("h_ev"), n - 1)
                nc.tensor.matmul(pv[b][0:NP, 0:C], hT[b][:, 0, 0:NP], w1a[:, :], start=True, stop=False)
                nc.tensor.matmul(pv[b][0:NP, 0:C], hT[b][:, 1, 0:NP], wew[:, :], start=False, stop=True)\
                    .then_inc(s("h_mm"), 1)
            pairs(pe, node1, 0, NT // 2)

            def item2(n, b, it):
                after(pe, s("sel2"), n)
                pe.wait_ge(s(f"g2{b}"), it * 16 * J + 16 * J)
                after(pe, s("z_add"), n, 2)
                for j in range(J):
                    ins = nc.tensor.matmul(pv[b][:, 0:C], SEL[b][:, j, :], V[b][:, j, 0:C],
                                           start=(j == 0), stop=(j == J - 1))
                ins.then_inc(s("vm2"), 1)
            pairs(pe, item2, 0, NG // 2)

            def node2(t, b, it):
                after(pe, s("zc_r"), t)
                after(pe, s("zc_u"), t, 2)
                nc.tensor.transpose(pt[b][:, 0:NP], hb[b][0:NP, 0, :], ident[0:NP, 0:NP]).then_inc(s("zc_t"), 1)
                after(pe, s("zc_u"), t)
                after(pe, s("zc_o"), t, 2)
                nc.tensor.matmul(pv[b][0:NP, 0:C], hT[b][:, 0, 0:NP], w2s[:, :], start=True, stop=True)\
                    .then_inc(s("zc_m"), 1)
            pairs(pe, node2, 0, NT // 2)

        @block.vector
        def _(dve):
            v = nc.vector
            count = [0]

            def link(ins):
                count[0] += 1
                ins.then_inc(s("chain"), 1)
                dve.wait_ge(s("chain"), count[0])

            def row(t3, t, lo, hi):
                return t3[0:NP, bass.DynSlice(t, 1), lo:hi].rearrange("p a c -> p (a c)")

            def layernorm(k, off):
                with dve.Fori(0, NT // 5) as it:
                    for q in range(5):
                        t = it * 5 + q
                        v.bn_stats(row(stat, t, 0, 6), row(xs, t, 0, C)).then_inc(s("stats"), 1)
                dve.wait_ge(s("stats"), k * NT)
                m_e, q_e = stat[0:NP, :, 1], stat[0:NP, :, 2]
                m_o, q_o = stat[0:NP, :, 4], stat[0:NP, :, 5]
                w0, w1, w2, w3 = (lnw[0:NP, i, :] for i in range(4))
                link(v.tensor_tensor(w2, m_e, m_o, ALU.subtract))
                link(v.tensor_tensor(w2, w2, w2, ALU.mult))
                link(v.tensor_tensor(w3, q_e, q_o, ALU.add))
                link(v.tensor_scalar(w2, w2, 0.25, None, ALU.mult))
                v.scalar_tensor_tensor(out=w0, in0=w3, scalar=1.0 / C, in1=w2, op0=ALU.mult,
                                       op1=ALU.add).then_inc(s("ln_a"), 1)
                dve.wait_ge(s("ln_a"), k)
                link(v.tensor_tensor(w3, m_e, m_o, ALU.add))
                dve.wait_ge(s("ln_sq"), k)
                link(v.reciprocal(rstd[0:NP, :], w1))
                v.scalar_tensor_tensor(out=nmr[0:NP, :], in0=w3, scalar=-0.5, in1=rstd[0:NP, :],
                                       op0=ALU.mult, op1=ALU.mult).then_inc(s("ln_b"), 1)

            dve.wait_ge(s("consts_in"), 16 * CONSTS)
            v.tensor_copy(beb[:, :], bes[:, 0:1].to_broadcast([128, 128])).then_inc(s("beb_done"), 1)
            dve.wait_ge(s("x_in"), 32)
            layernorm(1, 0)
            dve.wait_ge(s("idx_dst"), 32)
            link(v.tensor_copy(dd[:, :, :], dsti[:, :, :]))
            v.tensor_scalar(dd[0:DUP, NG - 1, :], dd[0:DUP, NG - 1, :], FAR, None, ALU.add).then_inc(s("d_f"), 2)
            dve.wait_ge(s("d_f"), 2)
            dve.wait_ge(s("shifted"), 5)
            dve.wait_ge(s("pool_c"), 20)
            prev, nxt = pa[0][:, 0:NG], pa[0][:, 128:128 + NG]
            v.tensor_copy(firsts[:, :], pa[0][:, 256:256 + NG]).then_inc(s("masks"), 1)
            v.tensor_copy(basei[0:1, :], pa[0][0:1, 256:256 + NG]).then_inc(s("base_i"), 1)
            v.tensor_copy(lasts[:, :], pa[0][:, 384:384 + NG]).then_inc(s("masks"), 1)
            v.tensor_tensor(isl[:, :, 0:J - 1], dd[:, :, 0:J - 1], dd[:, :, 1:J], ALU.not_equal)\
                .then_inc(s("masks"), 1)
            v.scalar_tensor_tensor(out=isl[:, :, J - 1], in0=nxt, scalar=edgefix[:, 1:2], in1=dd[:, :, J - 1],
                                   op0=ALU.add, op1=ALU.not_equal).then_inc(s("masks"), 1)
            v.tensor_tensor(cont[:, :, 1:J], dd[:, :, 0:J - 1], dd[:, :, 1:J], ALU.not_equal)\
                .then_inc(s("masks"), 1)
            v.memset(cont[:, :, 0:1], 1.0).then_inc(s("masks"), 1)
            v.scalar_tensor_tensor(out=cin[:, :], in0=prev, scalar=edgefix[:, 0:1], in1=dd[:, :, 0],
                                   op0=ALU.add, op1=ALU.not_equal).then_inc(s("masks"), 1)
            v.scalar_tensor_tensor(out=thru[:, :], in0=prev, scalar=edgefix[:, 0:1], in1=dd[:, :, J - 1],
                                   op0=ALU.add, op1=ALU.not_equal).then_inc(s("masks"), 1)
            dve.wait_ge(s("masks"), 8)
            for m in (cont[:, :, :], cin[:, :], thru[:, :]):
                v.tensor_scalar(m, m, -BIG, None, ALU.mult).then_inc(s("masks"), 1)
            v.tensor_tensor(drel[:, :, :], dd[:, :, :], firsts[:, :].rearrange("p (g a) -> p g a", a=1)
                            .to_broadcast([128, NG, J]), ALU.subtract).then_inc(s("masks"), 1)
            dve.wait_ge(s("masks"), 12)

            def node0(t, b, it):
                after(dve, s("h_tr"), t)
                after(dve, s("h_mm"), t, 2)
                v.tensor_copy(hT[b][:, 0, 0:NP], pt[b][:, 0:NP]).then_inc(s("h_trc"), 1)
                after(dve, s("h_mm"), t)
                v.tensor_copy(row(tab, t, 0, TW), pv[b][0:NP, 0:TW]).then_inc(s("h_ev"), 1)
            pairs(dve, node0, 0, NT // 2)
            dve.wait_ge(s("h_ev"), NT)
            dl = tab[0:NP, :, TAB:TW]
            dp = [dlog[0:NP, :, H:DL].bitcast(BF16)[:, :, k * H:(k + 1) * H] for k in range(NK)]
            v.tensor_copy(dlog[0:NP, :, 0:H], dl).then_inc(s("dl"), 1)
            v.tensor_copy(dp[0], dl).then_inc(s("dl"), 1)
            dve.wait_ge(s("dl"), 2)
            v.tensor_tensor(dres[0:NP, :, :], dl, dp[0], ALU.subtract).then_inc(s("dl"), 1)
            dve.wait_ge(s("dl"), 3)
            v.tensor_copy(dp[1], dres[0:NP, :, :]).then_inc(s("dl"), 1)
            dve.wait_ge(s("dl"), 4)
            v.tensor_tensor(dp[2], dres[0:NP, :, :], dp[1], ALU.subtract).then_inc(s("dl"), 1)
            dve.wait_ge(s("dl"), 5)
            v.memset(tab[0:NP, :, TAB - 1:TAB], 1.0).then_inc(s("tab_done"), 1)

            dve.wait_ge(s("iota_p"), 1)

            def select(n, b, name):
                v.tensor_tensor(SEL[b], iotap.rearrange("p (a w) -> p a w", a=1).to_broadcast([128, J, WIN]),
                                drel[:, bass.DynSlice(n, 1), :].rearrange("p a (j c) -> p (a j) c", c=1)
                                .to_broadcast([128, J, WIN]), ALU.is_equal).then_inc(s(name), 1)

            def split(n, full, rest, part, sems):
                known, s_rest, *s_part = sems
                after(dve, s(known), n)
                v.tensor_copy(part[0], full).then_inc(s(s_part[0]), 1)
                after(dve, s(s_part[0]), n)
                v.tensor_tensor(rest, full, part[0], ALU.subtract).then_inc(s(s_rest), 1)
                after(dve, s(s_rest), n)
                v.tensor_copy(part[1], rest).then_inc(s(s_part[1]), 1)
                after(dve, s(s_part[1]), n)
                v.tensor_tensor(part[2], rest, part[1], ALU.subtract).then_inc(s(s_part[2]), 1)

            def merge(n, b):
                dve.wait_ge(s("s_load"), n * 16 + 16)
                after(dve, s("fold_b"), n)
                st4 = state[:, 0:C].rearrange("p (h f) -> p h f", f=F)
                v.tensor_tensor(st4, st4, fold[b][:, :].rearrange("p (h a) -> p h a", a=1)
                                .to_broadcast([128, H, F]), ALU.mult).then_inc(s("ms_b"), 1)
                v.tensor_tensor(state[:, C:C + H], state[:, C:C + H], fold[b][:, :], ALU.mult)\
                    .then_inc(s("mt_b"), 1)
                after(dve, s("am_b"), n)
                v.tensor_tensor(state[:, TAB:ST], state[:, TAB:ST], pa[b][:, 0:C], ALU.add)\
                    .then_inc(s("mu_b"), 1)
                dve.wait_ge(s("vm_b"), n * 4 + 4)
                after(dve, s("ms_b"), n)
                after(dve, s("mt_b"), n)
                after(dve, s("mu_b"), n)
                v.tensor_tensor(state[:, 0:TAB], state[:, 0:TAB], pv[0][:, 0:TAB], ALU.add)\
                    .then_inc(s("merged"), 1)

            def item(n, b, it):
                if not (isinstance(n, int) and n < 2):
                    dve.wait_ge(s("vm_b"), n * 4 - 4)
                select(n, b, "sel_b")
                after(dve, s("thruT_b"), n, 1)
                v.tensor_copy(thru4[b][:, :], thru[:, bass.DynSlice(n, 1)].to_broadcast([128, H]))\
                    .then_inc(s("thru4_b"), 1)
                v.tensor_copy(cont4[:, :, :], cont[:, bass.DynSlice(n, 1), :].to_broadcast([128, H, J]))\
                    .then_inc(s("cont_b"), 1)
                dve.wait_ge(s(f"gat{b}"), it * 16 * J + 16 * J)
                v.tensor_copy(logit[:, :, :], V[b][:, :, C:C + H].rearrange("p j h -> p h j"))\
                    .then_inc(s("log_b"), 1)
                after(dve, s("cont_b"), n)
                after(dve, s("log_b"), n)
                flat = "p h j -> p (h j)"
                v.tensor_tensor_scan(pre1[:, :, :].rearrange(flat), cont4[:, :, :].rearrange(flat),
                                     logit[:, :, :].rearrange(flat), -BIG, ALU.add, ALU.max)\
                    .then_inc(s("pre1_b"), 1)
                after(dve, s("thru_c"), n)
                after(dve, s("tailT_b"), n)
                v.tensor_tensor_scan(tails[:, 1:129], thruT[:, :], tailT, -BIG, ALU.add, ALU.max)\
                    .then_inc(s("tails_b"), 1)
                after(dve, s("cback_b"), n)
                v.scalar_tensor_tensor(out=logit[:, :, 0], in0=cback, scalar=cin[:, bass.DynSlice(n, 1)],
                                       in1=logit[:, :, 0], op0=ALU.add, op1=ALU.max).then_inc(s("carry_b"), 1)
                after(dve, s("carry_b"), n)
                v.tensor_tensor_scan(pre2[:, :, :].rearrange(flat), cont4[:, :, :].rearrange(flat),
                                     logit[:, :, :].rearrange(flat), -BIG, ALU.add, ALU.max)\
                    .then_inc(s("pre2_b"), 1)
                last = isl[:, bass.DynSlice(n, 1), :].rearrange("p a (j c) -> p (a j) c", c=1)
                v.tensor_copy(peaks[:, :, NK * H:NK * H + 1], last).then_inc(s("pkl_b"), 1)
                after(dve, s("pre2_b"), n)
                v.tensor_tensor(pkf[:, :, :], pre2[:, :, :].rearrange("p h j -> p j h"),
                                last.to_broadcast([128, J, H]), ALU.mult).then_inc(s("pkf_b"), 1)
                split(n, pkf[:, :, :], pkr[:, :, :], [peaks[:, :, k * H:(k + 1) * H] for k in range(NK)],
                      ("pkf_b", "pr_b", "pk_b", "pk1_b", "pk2_b"))
                if not (isinstance(n, int) and n == 0):
                    merge(n - 1, 1 - b)
                after(dve, s("mg_b"), n)
                v.tensor_scalar(pen[:, :], mg[:, NK * H:NK * H + 1], -1.0, BIG, ALU.add, ALU.mult)\
                    .then_inc(s("pen_b"), 1)
                v.tensor_reduce(mgs[:, :], mg[:, 0:NK * H].rearrange("p (k h) -> p h k", h=H),
                                AX.X, ALU.add).then_inc(s("mgs_b"), 1)
                dve.wait_ge(s("st_load"), n * 32 + 32)
                after(dve, s("pen_b"), n)
                after(dve, s("mgs_b"), n)
                v.scalar_tensor_tensor(out=newold[b][:, 0, :], in0=mgs[:, :], scalar=pen[:, 0:1],
                                       in1=newold[b][:, 1, :], op0=ALU.add, op1=ALU.max)\
                    .then_inc(s("mnew_b"), 1)
                after(dve, s("mnew_b"), n)
                v.tensor_tensor(nu[:, :].rearrange("p (a h) -> p a h", h=H), newold[b][:, :, :],
                                node[b][:, 0:H].rearrange("p (a h) -> p a h", a=1).to_broadcast([128, 2, H]),
                                ALU.add).then_inc(s("nu_b"), 1)
                after(dve, s("nu_b"), n)
                v.scalar_tensor_tensor(out=node[b][:, SH:SH + 2 * H], in0=nu[:, :], scalar=SLOPE, in1=nu[:, :],
                                       op0=ALU.mult, op1=ALU.max).then_inc(s("node_b"), 1)
                split(n, node[b][:, SH:SH + H], shr[:, :],
                      [parts[b][:, (NK + k) * H:(NK + k + 1) * H] for k in range(NK)],
                      ("node_b", "sr_b", "sh0_b", "sh1_b", "sh2_b"))
                v.tensor_tensor(fd[:, :], node[b][:, SH + H:SH + 2 * H], node[b][:, SH:SH + H], ALU.subtract)\
                    .then_inc(s("fd_b"), 1)
                after(dve, s("look"), n)
                v.tensor_reduce(lks[:, :, :].rearrange("p j (g h) -> p (j g) h", h=H),
                                lk.rearrange("p j (g k h) -> p (j g) h k", k=NK, h=H), AX.X, ALU.add)\
                    .then_inc(s("lks_b"), 1)
                after(dve, s("lks_b"), n)
                v.tensor_tensor(lin[:, :, :], V[b][:, :, C:C + H], lks[:, :, 0:H], ALU.add).then_inc(s("lin_b"), 1)
                after(dve, s("lin_b"), n)
                v.scalar_tensor_tensor(out=lre[:, :, :], in0=lin[:, :, :], scalar=SLOPE, in1=lin[:, :, :],
                                       op0=ALU.mult, op1=ALU.max).then_inc(s("lre_b"), 1)
                after(dve, s("lre_b"), n)
                v.tensor_tensor(lin[:, :, :], lre[:, :, :], lks[:, :, H:2 * H], ALU.subtract)\
                    .then_inc(s("zs_b"), 1)
                after(dve, s("zs_b"), n)
                v.tensor_scalar(lre[:, :, :], lin[:, :, :], 0.0, None, ALU.min).then_inc(s("zm_b"), 1)
                after(dve, s("wp_b"), n)
                for q in range(4):
                    js = slice(q * QUART, (q + 1) * QUART)
                    v4 = V[b][:, js, 0:C].rearrange("p j (h f) -> p j h f", f=F)
                    v.tensor_tensor(v4, v4, wps[:, js, :].rearrange("p j (h a) -> p j h a", a=1)
                                    .to_broadcast([128, QUART, H, F]), ALU.mult).then_inc(s("vw_b"), 1)
            pairs(dve, item, 0, NG // 2)
            merge(NG - 1, 1)

            dve.wait_ge(s("sum_in"), 32)
            dn = allsum[0:NP, :, C:C + H]
            link(v.reciprocal(rden[0:NP, :, :], dn))
            for h in range(H):
                part = allsum[0:NP, :, h * F:(h + 1) * F]
                link(v.tensor_tensor(part, part, rden[0:NP, :, h:h + 1].to_broadcast([NP, NT, F]), ALU.mult))
            full = allsum[0:NP, :, 0:C]
            link(v.tensor_tensor(full, full, b0s[0:NP, :].rearrange("p (a c) -> p a c", a=1)
                                 .to_broadcast([NP, NT, C]), ALU.add))
            link(v.scalar_tensor_tensor(out=xs[0:NP, :, :], in0=full, scalar=0.0, in1=xs[0:NP, :, :],
                                        op0=ALU.max, op1=ALU.add))
            layernorm(2, NT)

            def node1(t, b, it):
                n = t + NT
                dve.wait_ge(s("h_tr"), n + 1)
                dve.wait_ge(s("h_mm"), n - 1)
                v.tensor_copy(hT[b][:, :, 0:NP], pt[b][:, 0:256].rearrange("p (a c) -> p a c", a=2)[:, :, 0:NP])\
                    .then_inc(s("h_trc"), 1)
                dve.wait_ge(s("h_mm"), n + 1)
                v.scalar_tensor_tensor(out=row(tab, t, 0, C), in0=bew[0:NP, :],
                                       scalar=row(allsum, t, TAB - 1, TAB), in1=pv[b][0:NP, 0:C],
                                       op0=ALU.mult, op1=ALU.add).then_inc(s("h_ev"), 1)
            pairs(dve, node1, 0, NT // 2)
            dve.wait_ge(s("h_ev"), 2 * NT)
            v.tensor_copy(pen[:, :], b1s[:, :]).then_inc(s("tab1_done"), 1)
            v.tensor_tensor(xs[0:NP, :, :], xs[0:NP, :, :], b2s[0:NP, :].rearrange("p (a c) -> p a c", a=1)
                            .to_broadcast([NP, NT, C]), ALU.add).then_inc(s("b2add"), 1)

            def item2(n, b, it):
                after(dve, s("vm2"), n, 2)
                select(n, b, "sel2")
                dve.wait_ge(s("z_load"), n * 16 + 16)
                after(dve, s("vm2"), n)
                v.tensor_tensor(state[:, 0:C], state[:, 0:C], pv[b][:, 0:C], ALU.add).then_inc(s("z_add"), 1)
            pairs(dve, item2, 0, NG // 2)

            dve.wait_ge(s("b2add"), 1)

            def node2(t, b, it):
                after(dve, s("zc_m"), t)
                v.tensor_tensor(row(tab, t, 0, C), pv[b][0:NP, 0:C], row(xs, t, 0, C), ALU.add)\
                    .then_inc(s("zc_o"), 1)
            pairs(dve, node2, 0, NT // 2)


CONSTS = 1 + 2 * H + 4 + 2 + 2
PADS = 0
for _wd in (DL, H, ST, C):
    PADS += -(-((NPAD - N) // 75 * _wd) // (ST - C - H))

_INS = ['x', 'src', 'dst', 'edge_attr_128', 'L0_gnn_W', 'L0_gnn_att_src', 'L0_gnn_att_dst', 'L0_gnn_bias',
        'L1_gnn_We', 'L1_gnn_be', 'L1_gnn_W1', 'L1_gnn_b1', 'L1_gnn_W2', 'L1_gnn_b2']


def kernel(**inputs):
    import numpy as _np
    import concourse.bacc as _bacc
    from concourse import mybir as _mybir
    from concourse.bass_utils import run_bass_kernel_spmd as _run

    nc = _bacc.Bacc("TRN2", target_bir_lowering=False, num_devices=1)
    arrays, args = {}, []
    for name in _INS:
        a = _np.ascontiguousarray(inputs[name])
        arrays[f"in_{name}_dram"] = a
        args.append(nc.dram_tensor(f"in_{name}_dram", a.shape, _mybir.dt.from_np(a.dtype), kind="ExternalInput").ap())
    args.append(nc.dram_tensor("out_0_dram", (N, C), _mybir.dt.float32, kind="ExternalOutput").ap())
    gnn_kernel(nc, *args)
    r = _run(nc, [arrays], core_ids=[0])
    return r.results[0]["out_0_dram"]
```

```python
import concourse.bass as bass
from concourse import mybir
from contextlib import ExitStack

FP32 = mybir.dt.float32
INT32 = mybir.dt.int32
BF16 = mybir.dt.bfloat16
ALU = mybir.AluOpType
ACT = mybir.ActivationFunctionType
AX = mybir.AxisListType

N = 6250
E = 200000
C = 128
H = 4
F = C // H
SLOPE = 0.2
EPS = 1e-5

NP = 125
NT = N // NP
SPLIT = 112

J = 16
GE = 128 * J
NG = -(-E // GE)
LAST = E - GE
DUP = (NG * GE - E) // J
assert DUP * J == NG * GE - E and NG % 2 == 0 and NP * NT == N
NQ = NT // 2
assert NT % 2 == 0 and NQ % 2 == 1
X_CHUNKS = ((0, 10), (10, 30), (30, NT))
TAB_CHUNKS = 5
assert NQ % TAB_CHUNKS == 0
WIN = 128
TOP = N - WIN
NPAD = N + 150
BIG = 1e30
FAR = 1e6

NX = 48
assert NX >= N // WIN and NX % 2 == 0
DUMMY = N

TAB = C + H + 1
TW = TAB + H
NK = 3
DL = H + NK * H // 2
QUART = J // 4
FIN = 18
MAGIC = 0x5f3759df
ST = TAB + C


def gnn_kernel(nc, x, src, dst, attr, W, att_src, att_dst, bias0, We, be, W1, b1, W2, b2, out):
    ctx = ExitStack()
    with ctx:
        def sb(name, shape, dt=FP32):
            return ctx.enter_context(nc.sbuf_tensor(name, shape, dt))

        def sem(name):
            return ctx.enter_context(nc.semaphore(name))

        def dram(name, shape):
            return nc.dram_tensor(name, shape, FP32, kind="Internal").ap()

        table0 = dram("table0", [N, TAB])
        table1 = dram("table1", [N, C])
        dlogit = dram("dlogit", [NPAD, DL])
        peak = dram("peak", [NPAD, H])
        sums0 = dram("sums0", [NPAD, ST])
        sums1 = dram("sums1", [NPAD, C])
        resid = dram("resid", [N, C])

        xs = sb("xs", [128, NT, C])
        unit = sb("unit", [128, TW])
        tab = sb("tab", [128, NT, TW])
        big = sb("big", [128, NT * ST])
        V = [big[:, b * J * TAB:(b + 1) * J * TAB].rearrange("p (j c) -> p j c", c=TAB) for b in range(2)]
        o = 2 * J * TAB
        AT = [big[:, o + b * J * C:o + (b + 1) * J * C].rearrange("p (j c) -> p j c", c=C) for b in range(2)]
        o += 2 * J * C
        SEL = [big[:, o + b * J * WIN:o + (b + 1) * J * WIN].rearrange("p (j w) -> p j w", w=WIN)
               for b in range(2)]
        assert o + 2 * J * WIN <= NT * ST
        allsum = big[:, :].rearrange("p (t c) -> p t c", c=ST)
        zin = big[:, 0:NT * C].rearrange("p (t c) -> p t c", c=C)
        selH = sb("selH", [128, J, WIN], BF16)
        selT = sb("selT", [128, J * 128], BF16)
        identH = sb("identH", [128, 128], BF16)
        dlog = sb("dlog", [128, NT, DL])
        dres = sb("dres", [128, NT, H])
        dsti = sb("dsti", [128, NG, J], INT32)
        dd = sb("dd", [128, NG, J])
        drel = sb("drel", [128, NG, J])
        cont = sb("cont", [128, NG, J])
        isl = sb("isl", [128, NG, J])
        cin = sb("cin", [128, NG])
        thru = sb("thru", [128, NG])
        firsts = sb("firsts", [128, NG])
        lasts = sb("lasts", [128, NG])
        basei = sb("basei", [1, NG], INT32)
        spani = sb("spani", [128, NG], INT32)
        wins = sb("wins", [128, NG])
        upto = sb("upto", [128, NG])
        onef = sb("onef", [128, NG])
        before = sb("before", [128, NG])
        extw = sb("extw", [128, NG])
        extc = sb("extc", [128, 8])
        rank = sb("rank", [128, 1])
        extd = sb("extd", [128, 128])
        ones = sb("ones", [128, 128])
        extb = sb("extb", [128, 128])
        extrow = [sb(f"extrow{i}", [1, 128], INT32) for i in range(3)]
        extn = sb("extn", [1, 1], INT32)
        drx = [sb(f"drx{b}", [128, J]) for b in range(2)]
        idx = [sb(f"idx{b}", [128, J], INT32) for b in range(2)]
        idx2 = [sb(f"idx2{b}", [128, J], INT32) for b in range(2)]
        iotaf = sb("iotaf", [128, 128])
        ident = sb("ident", [128, 128])
        shp = sb("shp", [128, 128])
        shn = sb("shn", [128, 128])
        pick = [sb(f"pick{i}", [128, 128]) for i in range(3)]
        edgefix = sb("edgefix", [128, 2])
        wcat = sb("wcat", [128, TW])
        wT = sb("wT", [128, 128])
        weT = sb("weT", [128, 128])
        attm = sb("attm", [128, 2 * H + 1])
        wes = sb("wes", [128, C])
        w1a = sb("w1a", [128, C])
        w1b = sb("w1b", [128, C])
        wew = sb("wew", [128, C])
        w2s = sb("w2s", [128, C])
        bes = sb("bes", [128, 1])
        beb = sb("beb", [128, 128])
        bew = sb("bew", [128, C])
        b0s = sb("b0s", [128, C])
        b2s = sb("b2s", [128, C])
        b1s = sb("b1s", [128, 1])
        init = sb("init", [128, ST - C])
        stat = sb("stat", [128, NT, 6])
        lnw = sb("lnw", [128, 4, NT])
        rstd = sb("rstd", [128, NT])
        nmr = sb("nmr", [128, NT])
        epsc = sb("epsc", [128, 1])
        rden = sb("rden", [128, NT, H])
        hb = [sb(f"hb{b}", [128, 2, 128]) for b in range(2)]
        hT = [sb(f"hT{b}", [128, 2, 128]) for b in range(2)]
        cont4 = sb("cont4", [128, H, J])
        logit = sb("logit", [128, H, J])
        pre1 = sb("pre1", [128, H, J])
        pre2 = sb("pre2", [128, H, J])
        thru4 = [sb(f"thru4{b}", [128, H]) for b in range(2)]
        thruT = sb("thruT", [H, 128])
        tails = sb("tails", [H, 129])
        pkf = sb("pkf", [128, J, H])
        pkr = sb("pkr", [128, J, H])
        peaks = sb("peaks", [128, J, NK * H + 1], BF16)
        mgs = sb("mgs", [128, H])
        shr = sb("shr", [128, H])
        lks = sb("lks", [128, J, 2 * H])
        pen = sb("pen", [128, 1])
        newold = [sb(f"newold{b}", [128, 2, H]) for b in range(2)]
        node = [sb(f"node{b}", [128, DL + NK * H // 2 + 2 * H]) for b in range(2)]
        SH = DL + NK * H // 2
        parts = [node[b][:, H:SH].bitcast(BF16) for b in range(2)]
        fold = [sb(f"fold{b}", [128, H]) for b in range(2)]
        lin = sb("lin", [128, J, H])
        lre = sb("lre", [128, J, H])
        state = sb("state", [128, ST])
        nu = sb("nu", [128, 2 * H])
        fxw = sb("fxw", [128, C])
        frd = sb("frd", [128, H])
        fo = sb("fo", [128, C])
        fx = sb("fx", [128, C])
        fxb = sb("fxb", [128, C])
        fdeg = sb("fdeg", [128, 1])
        fst = sb("fst", [128, 6])
        fmv = sb("fmv", [128, 2])
        fve = sb("fve", [128, 1])
        fy0 = sb("fy0", [128, 1])
        fy1 = sb("fy1", [128, 1])
        fnm = sb("fnm", [128, 1])
        fh = sb("fh", [128, C])
        fhT = sb("fhT", [128, 2 * C])
        fy = sb("fy", [128, C])
        flag = sb("flag", [1, 5])
        fd = sb("fd", [128, H])

        def bank(name):
            return ctx.enter_context(nc.psum_tensor(name, [128, 512], FP32))
        pv = [bank(f"pv{b}") for b in range(2)]
        pa = [bank(f"pa{b}") for b in range(2)]
        pt = [bank(f"pt{b}") for b in range(2)]
        pc = bank("pc")
        pm = bank("pm")
        iotap = pc[:, 0:128]
        tailT = pm[0:H, 0:128]
        thruP = pm[0:H, 128:256]
        cback = pm[:, 256:256 + H]
        mg = pm[:, 264:264 + NK * H + 1]
        lk = pa[0][:, 0:2 * NK * H * J].rearrange("p (j c) -> p j c", c=2 * NK * H)
        sumV = [pv[b][:, 0:TAB] for b in range(2)]
        sumA = [pv[b][:, TAB:ST] for b in range(2)]
        sums = [pv[b][:, 0:ST] for b in range(2)]
        finT = pa[1][:, 0:2 * C]
        finY = pa[1][:, 256:256 + C]
        ptH = [pt[b][:, :].bitcast(BF16) for b in range(2)]
        wps = pm[:, 400:400 + H * J].rearrange("p (j c) -> p j c", c=H)

        S = {}

        def s(name):
            if name not in S:
                S[name] = sem(name)
            return S[name]

        names = """x_in0 x_in1 x_in2 idx_dst consts_in prep pool_c unit_z iota_p pad_z pad_out rank_b
            w_t w_tc w_aux w_auxc beb_done stats chain ln_a ln_sq ln_b h_ready h_tr h_trc h_mm h_ev
            split_dd d_f pmasks shifted masks base_i ext ext_cols ext_mm ext_done
            dl dl_done tab0_out peak_out tab_out sp_turn
            idx0 idx1 gat0 gat1 attr0 attr1 g_started st_load m_store s_load s_store xw_load
            sel_b drx_b selh_b thru4_b thruT_b thru_c cont_b log_b pre1_b tailT_b tails_b cback_b carry_b pre2_b
            pkl_b pkf_b pk_b pr_b pk1_b pk2_b mg_b pen_b mgs_b mnew_b nu_b node_b sh0_b sr_b sh1_b sh2_b
            fd_b fold_b sttr stcp look lks_b lin_b lre_b zs_b zm_b w_b wp_b vw_b am_b vm_b ms_b mt_b merged
            fin fin_turn x1_f nmr_f h_f ftr_f ht_f ym_f y_f xb_f xb_out y_out
            sum_in y_ready tab1_done tab1_out sum1_out
            i20 i21 g20 g21 g2_started sel2 drx2_b vm2 z_load z_add z_store xr_load zt_f zu_f zy_f zo_f z_out
            z_in zc_r zc_t zc_u zc_m zc_o out_w b2add""".split()
        for n_ in names:
            s(n_)

        block = ctx.enter_context(nc.Block())

        def nodes(ap, width_from, width_to):
            return ap[0:N, width_from:width_to].rearrange("(p t) c -> p t c", t=NT)

        def after(eng, sm, n, lag=0):
            if isinstance(n, int) and n - lag < 0:
                return
            eng.wait_ge(sm, n + (1 - lag))

        def after_dma(eng, sm, count):
            if isinstance(count, int) and count <= 0:
                return
            eng.wait_ge(sm, count * 16)

        def pairs(eng, body, count):
            for b in range(2):
                body(b, b, 0)
            with eng.Fori(1, count) as it:
                for b in range(2):
                    body(it * 2 + b, b, it)

        def uncovered(eng):
            eng.wait_ge(s("ext_done"), 5)
            return eng.value_load(extn[0:1, 0:1], min_val=0, max_val=N)

        def extra_pairs(eng, body):
            with eng.Fori(NG // 2, NG // 2 + NX // 2) as it:
                for b in range(2):
                    body(it * 2 + b, b, it)

        def extra(eng, what, n, most):
            return eng.value_load(extrow[what][0:1, bass.DynSlice(n - NG, 1)], min_val=0, max_val=most)

        @block.sync
        def _(sp):
            for i, (first, end) in enumerate(X_CHUNKS):
                for lo, hi in ((0, SPLIT), (SPLIT, NP)):
                    sp.dma_start(xs[lo:hi, first:end, :], nodes(x, 0, C)[lo:hi, first:end, :])\
                        .then_inc(s(f"x_in{i}"), 16)
            sp.wait_ge(s("prep"), 1)
            sp.dma_start(wcat[:, 0:C], W).then_inc(s("consts_in"), 16)
            for h in range(H):
                sp.dma_start(attm[h * F:(h + 1) * F, h:h + 1],
                             att_src[h, :].rearrange("(f a) -> f a", a=1)).then_inc(s("consts_in"), 16)
                sp.dma_start(attm[h * F:(h + 1) * F, H + 1 + h:H + 2 + h],
                             att_dst[h, :].rearrange("(f a) -> f a", a=1)).then_inc(s("consts_in"), 16)
            sp.dma_start(wes[:, :], We).then_inc(s("consts_in"), 16)
            sp.dma_start(w1a[:, :], W1[0:C, :]).then_inc(s("consts_in"), 16)
            sp.dma_start(w1b[:, :], W1[C:2 * C, :]).then_inc(s("consts_in"), 16)
            sp.dma_start(w2s[:, :], W2).then_inc(s("consts_in"), 16)
            sp.dma_start(bes[:, :], be.rearrange("(p a) -> p a", a=1)).then_inc(s("consts_in"), 16)
            sp.dma_start(b1s[:, :], b1.rearrange("(p a) -> p a", a=1)).then_inc(s("consts_in"), 16)
            sp.dma_start(b0s[:, :], bias0.rearrange("(a n) -> a n", a=1).to_broadcast([128, C]))\
                .then_inc(s("consts_in"), 16)
            sp.dma_start(b2s[:, :], b2.rearrange("(a n) -> a n", a=1).to_broadcast([128, C]))\
                .then_inc(s("consts_in"), 16)
            sp.dma_start(dsti[:, 0:NG - 1, :],
                         dst[0:(NG - 1) * GE].rearrange("(g p j) -> p g j", p=128, j=J))\
                .then_inc(s("idx_dst"), 16)
            sp.dma_start(dsti[:, NG - 1, :], dst[LAST:E].rearrange("(p j) -> p j", j=J))\
                .then_inc(s("idx_dst"), 16)

            sp.wait_ge(s("pad_z"), 1)
            pads = NPAD - N
            zero = init[:, H:H + 1]
            for ap, wd in ((dlogit, DL), (peak, H), (sums0, ST), (sums1, C)):
                rows = ap[N:NPAD, :].rearrange("(p q) c -> p (q c)", p=75)
                n_el = pads // 75 * wd
                done = 0
                while done < n_el:
                    k = min(n_el - done, ST - C - H)
                    sp.dma_start(rows[:, done:done + k], init[0:75, H:H + k]).then_inc(s("pad_out"), 16)
                    done += k

            def load_edges(n, b, it, start):
                after_dma(sp, s(f"gat{b}"), it * J)
                sp.sem_inc(s("sp_turn"), 1)
                sp.dma_start(idx[b][:, :], src[bass.DynSlice(start, GE)].rearrange("(p j) -> p j", j=J))\
                    .then_inc(s(f"idx{b}"), 16)
                after(sp, s("am_b"), n, 2)
                sp.dma_start(AT[b], attr[bass.DynSlice(start, GE), :].rearrange("(p j) c -> p j c", j=J))\
                    .then_inc(s(f"attr{b}"), 16)

            sp.sem_inc(s("y_out"), 16)
            for b in range(2):
                load_edges(b, b, 0, b * GE)

            for lo, hi in ((0, SPLIT), (SPLIT, NP)):
                sp.dma_start(nodes(sums0, C, ST)[lo:hi],
                             init[lo:hi, :].rearrange("p (a c) -> p a c", a=1).to_broadcast([hi - lo, NT, ST - C]))\
                    .then_inc(s("tab_out"), 16)

            for i in range(TAB_CHUNKS):
                sp.wait_ge(s("h_ev"), NQ // TAB_CHUNKS * (i + 1))
                ts = slice(NT // TAB_CHUNKS * i, NT // TAB_CHUNKS * (i + 1))
                for lo, hi in ((0, SPLIT), (SPLIT, NP)):
                    sp.dma_start(nodes(table0, 0, TAB)[lo:hi, ts, :], tab[lo:hi, ts, 0:TAB])\
                        .then_inc(s("tab0_out"), 16)
                for lo, hi in ((0, SPLIT), (SPLIT, NP)):
                    sp.dma_start(nodes(sums0, 0, C)[lo:hi, ts, :], tab[lo:hi, ts, 0:C]).then_inc(s("tab_out"), 16)
            sp.wait_ge(s("dl_done"), 1)
            sp.wait_ge(s("tab0_out"), 32 * TAB_CHUNKS)
            for lo, hi in ((0, SPLIT), (SPLIT, NP)):
                sp.dma_start(nodes(dlogit, 0, DL)[lo:hi], dlog[lo:hi, :, :]).then_inc(s("peak_out"), 16)
                sp.dma_start(nodes(peak, 0, H)[lo:hi], tab[lo:hi, :, C:C + H]).then_inc(s("peak_out"), 16)

            def load_peak(n, b, base):
                after_dma(sp, s("m_store"), n)
                sp.dma_start(newold[b][:, 1, :], peak[bass.DynSlice(base, WIN), :]).then_inc(s("st_load"), 16)
                sp.dma_start(node[b][:, 0:DL], dlogit[bass.DynSlice(base, WIN), :]).then_inc(s("st_load"), 16)

            def store_peak(n, b, base):
                after(sp, s("mnew_b"), n)
                sp.dma_start(peak[bass.DynSlice(base, WIN), :], newold[b][:, 0, :]).then_inc(s("m_store"), 16)

            def load_sums(n, base, is_extra=False):
                after_dma(sp, s("s_store"), n)
                if not is_extra:
                    after(sp, s("ftr_f"), n, 1)
                sp.dma_start(state[:, :], sums0[bass.DynSlice(base, WIN), :]).then_inc(s("s_load"), 16)
                if not is_extra:
                    after(sp, s("x1_f"), n, 1)
                    sp.dma_start(fxw[:, :], x[bass.DynSlice(base, WIN), :]).then_inc(s("xw_load"), 16)

            def store_sums(n, base):
                after(sp, s("merged"), n)
                sp.dma_start(sums0[bass.DynSlice(base, WIN), :], state[:, :]).then_inc(s("s_store"), 16)

            def store_residual(n, base):
                after_dma(sp, s("xb_out"), n)
                after(sp, s("xb_f"), n)
                sp.dma_start(resid[bass.DynSlice(base, WIN), :], fxb[:, :]).then_inc(s("xb_out"), 16)

            def store_projected(n, base):
                sp.wait_ge(s("y_out"), n * 32 + 16)
                after(sp, s("y_f"), n)
                sp.dma_start(table1[bass.DynSlice(base, WIN), :], fy[:, :]).then_inc(s("y_out"), 16)
                sp.dma_start(sums1[bass.DynSlice(base, WIN), :], fy[:, :]).then_inc(s("y_out"), 16)

            sp.wait_ge(s("base_i"), 1)
            sp.wait_ge(s("pad_out"), 16 * PADS)
            sp.wait_ge(s("peak_out"), 16 * 4)

            def base_of(g):
                return sp.value_load(basei[0:1, bass.DynSlice(g, 1)], min_val=0, max_val=TOP)

            def item(n, b, it):
                base = base_of(n)
                load_peak(n, b, base)
                before_first = isinstance(n, int) and n == 0
                if not before_first:
                    base_before = base_of(n - 1)
                    store_sums(n - 1, base_before)
                store_peak(n, b, base)
                if not isinstance(n, int) or n + 2 < NG - 1:
                    load_edges(n + 2, b, it + 1, (n + 2) * GE)
                elif n + 2 == NG - 1:
                    load_edges(n + 2, b, it + 1, LAST)
                if before_first:
                    sp.wait_ge(s("tab_out"), 32 * (TAB_CHUNKS + 1))
                load_sums(n, base)
                if not before_first:
                    store_residual(n - 1, base_before)
                if not (isinstance(n, int) and n < 2):
                    store_projected(n - 2, base_of(n - 2))

            for b in range(2):
                item(b, b, 0)
            with sp.Fori(1, NG // 2 - 2) as it:
                for b in range(2):
                    item(it * 2 + b, b, it)
            for it in range(NG // 2 - 2, NG // 2):
                for b in range(2):
                    item(it * 2 + b, b, it)
            def load_idx(n, b, it, start):
                after_dma(sp, s(f"g2{b}"), it * J)
                sp.sem_inc(s("sp_turn"), 1)
                sp.dma_start(idx2[b][:, :], src[bass.DynSlice(start, GE)].rearrange("(p j) -> p j", j=J))\
                    .then_inc(s(f"i2{b}"), 16)

            for b in range(2):
                load_idx(b, b, 0, b * GE)

            base = base_of(NG - 1)
            store_sums(NG - 1, base)
            store_projected(NG - 2, base_of(NG - 2))
            store_residual(NG - 1, base)
            store_projected(NG - 1, base)
            sp.wait_ge(s("xb_out"), 16 * NG)
            sp.wait_ge(s("y_out"), 32 * NG + 16)

            def extra_item(n, b, it):
                load_edges(n, b, it, extra(sp, 2, n, LAST))
                base = extra(sp, 1, n, N)
                load_peak(n, b, base)
                store_peak(n, b, base)
                load_sums(n, base, True)
                store_sums(n, base)
                sp.wait_ge(s("s_store"), n * 16 + 16)
                sp.sem_inc(s("sp_turn"), 1)

            with sp.If(uncovered(sp) > 0):
                extra_pairs(sp, extra_item)
                for lo, hi in ((0, SPLIT), (SPLIT, NP)):
                    sp.dma_start(allsum[lo:hi], nodes(sums0, 0, ST)[lo:hi]).then_inc(s("sum_in"), 16)
                sp.wait_ge(s("tab1_done"), 1)
                for ap, written in ((table1, "tab1_out"), (sums1, "sum1_out")):
                    for lo, hi in ((0, SPLIT), (SPLIT, NP)):
                        sp.dma_start(nodes(ap, 0, C)[lo:hi], tab[lo:hi, :, 0:C]).then_inc(s(written), 16)
                sp.wait_ge(s("sum1_out"), 32)
                sp.wait_ge(s("tab1_out"), 32)
                sp.sem_inc(s("sp_turn"), 1)

            def load_z(n, base, is_extra=False):
                after_dma(sp, s("z_store"), n)
                if not is_extra:
                    after(sp, s("zt_f"), n, 1)
                sp.dma_start(state[:, 0:C], sums1[bass.DynSlice(base, WIN), :]).then_inc(s("z_load"), 16)
                if not is_extra:
                    after(sp, s("zo_f"), n, 1)
                    sp.dma_start(fxw[:, :], resid[bass.DynSlice(base, WIN), :]).then_inc(s("xr_load"), 16)

            def store_z(n, base):
                after(sp, s("z_add"), n)
                sp.dma_start(sums1[bass.DynSlice(base, WIN), :], state[:, 0:C]).then_inc(s("z_store"), 16)

            def item2(n, b, it):
                if not isinstance(n, int) or n + 2 < NG - 1:
                    load_idx(n + 2, b, it + 1, (n + 2) * GE)
                elif n + 2 == NG - 1:
                    load_idx(n + 2, b, it + 1, LAST)
                base = base_of(n)
                load_z(n, base)
                store_z(n, base)
                after_dma(sp, s("z_out"), n)
                after(sp, s("zo_f"), n)
                sp.dma_start(out[bass.DynSlice(base, WIN), :], fy[:, :]).then_inc(s("z_out"), 16)

            for b in range(2):
                item2(b, b, 0)
            with sp.Fori(1, NG // 2 - 2) as it:
                for b in range(2):
                    item2(it * 2 + b, b, it)
            for it in range(NG // 2 - 2, NG // 2):
                for b in range(2):
                    item2(it * 2 + b, b, it)
            sp.wait_ge(s("z_out"), 16 * NG)

            def extra_item2(n, b, it):
                load_idx(n, b, it, extra(sp, 2, n, LAST))
                base = extra(sp, 1, n, N)
                load_z(n, base, True)
                store_z(n, base)
                sp.wait_ge(s("z_store"), n * 16 + 16)
                sp.sem_inc(s("sp_turn"), 1)

            with sp.If(uncovered(sp) > 0):
                extra_pairs(sp, extra_item2)
                for lo, hi in ((0, SPLIT), (SPLIT, NP)):
                    sp.dma_start(zin[lo:hi], nodes(sums1, 0, C)[lo:hi]).then_inc(s("z_in"), 16)
                sp.wait_ge(s("zc_o"), NT)
                for lo, hi in ((0, SPLIT), (SPLIT, NP)):
                    sp.dma_start(nodes(out, 0, C)[lo:hi], tab[lo:hi, :, 0:C]).then_inc(s("out_w"), 16)
                sp.wait_ge(s("out_w"), 32)
                sp.sem_inc(s("sp_turn"), 1)

        @block.gpsimd
        def _(pool):
            pool.memset(attm[:, :], 0.0).then_inc(s("prep"), 1)
            pool.memset(unit[:, 0:TAB - 1], 0.0).then_inc(s("unit_z"), 1)
            pool.memset(unit[:, TAB - 1:TAB], 1.0).then_inc(s("unit_z"), 1)
            pool.memset(unit[:, TAB:TW], 0.0).then_inc(s("unit_z"), 1)
            pool.memset(wcat[:, C:TW], 0.0).then_inc(s("pool_c"), 1)
            pool.memset(init[:, 0:H], 1.0).then_inc(s("pool_c"), 1)
            pool.memset(init[:, H:ST - C], 0.0).then_inc(s("pool_c"), 1)
            pool.wait_ge(s("pool_c"), 3)
            pool.iota(iotaf[:, :], [[1, 128]], base=0, channel_multiplier=0,
                      allow_small_or_imprecise_dtypes=True).then_inc(s("pad_z"), 1)
            pool.iota(rank[:, :], [[1, 1]], base=0, channel_multiplier=1,
                      allow_small_or_imprecise_dtypes=True).then_inc(s("rank_b"), 1)
            pool.memset(onef[:, :], 1.0).then_inc(s("rank_b"), 1)
            pool.memset(ones[:, :], 1.0).then_inc(s("rank_b"), 1)
            tiles = [(ident, 0, 1, [[-1, 128]]), (shp, 1, 1, [[-1, 128]]), (shn, -1, 1, [[-1, 128]]),
                     (pick[0], 0, 1, [[0, 128]]), (pick[1], -127, 1, [[0, 128]]), (pick[2], -DUP, 1, [[0, 128]])]
            for tl, _, _, _ in tiles:
                pool.memset(tl[:, :], 0.0).then_inc(s("pool_c"), 1)
            pool.memset(edgefix[:, :], 0.0).then_inc(s("pool_c"), 1)
            pool.memset(epsc[:, :], EPS).then_inc(s("pool_c"), 1)
            pool.memset(tails[:, :], -BIG).then_inc(s("pool_c"), 1)
            pool.wait_ge(s("pool_c"), 12)
            for tl, base, cm, pat in tiles:
                pool.affine_select(out=tl[:, :], in_=tl[:, :], compare_op=ALU.not_equal, fill=1.0,
                                   base=base, pattern=pat, channel_multiplier=cm).then_inc(s("pool_c"), 1)
            for c, base in ((0, 0), (1, -127)):
                pool.affine_select(out=edgefix[:, c:c + 1], in_=edgefix[:, c:c + 1], compare_op=ALU.not_equal,
                                   fill=-1.0, base=base, pattern=[[0, 1]], channel_multiplier=1)\
                    .then_inc(s("pool_c"), 1)

            pool.wait_ge(s("consts_in"), 16 * CONSTS)
            nc.gpsimd.tensor_copy(beb[:, :], bes[:, 0:1].to_broadcast([128, 128])).then_inc(s("beb_done"), 1)

            pool.wait_ge(s("idx_dst"), 32)
            nc.gpsimd.tensor_copy(dd[:, :, :], dsti[:, :, :]).then_inc(s("split_dd"), 1)
            pool.wait_ge(s("split_dd"), 1)
            nc.gpsimd.tensor_scalar(dd[0:DUP, NG - 1, :], dd[0:DUP, NG - 1, :], FAR, None, ALU.add)\
                .then_inc(s("d_f"), 2)
            pool.wait_ge(s("d_f"), 2)
            nc.gpsimd.tensor_tensor(isl[:, :, 0:J - 1], dd[:, :, 1:J], dd[:, :, 0:J - 1], ALU.subtract)\
                .then_inc(s("pmasks"), 1)
            pool.memset(cont[:, :, 0:1], -BIG).then_inc(s("pmasks"), 1)
            pool.wait_ge(s("pmasks"), 2)
            nc.gpsimd.tensor_scalar(cont[:, :, 1:J], isl[:, :, 0:J - 1], 1.0, -BIG, ALU.min, ALU.mult)\
                .then_inc(s("pmasks"), 1)
            pool.wait_ge(s("pmasks"), 3)
            nc.gpsimd.tensor_scalar(isl[:, :, 0:J - 1], isl[:, :, 0:J - 1], 1.0, None, ALU.min)\
                .then_inc(s("pmasks"), 1)

            def gather(b, it, rows, table, index, gat, ix, started, n=None):
                pool.wait_ge(s(f"{ix}{b}"), it * 16 + 16)
                pool.sem_inc(s(started), 1)
                for j in range(J):
                    if n is not None and j % QUART == 0 and not (isinstance(n, int) and n < 2):
                        pool.wait_ge(s("vm_b"), n * 4 + (j // QUART - 7))
                        pool.sem_inc(s(started), 1)
                    pool.indirect_dma_start(
                        out=V[b][:, j, 0:rows], out_offset=None, in_=table,
                        in_offset=bass.IndirectOffsetOnAxis(ap=index[b][:, j:j + 1], axis=0))\
                        .then_inc(s(f"{gat}{b}"), 16)

            pool.wait_ge(s("tab0_out"), 32 * TAB_CHUNKS)

            def item(n, b, it):
                gather(b, it, TAB, table0, idx, "gat", "idx", "g_started", n)
            pairs(pool, item, NG // 2)
            with pool.If(uncovered(pool) > 0):
                extra_pairs(pool, item)
                pool.wait_ge(s("tab1_out"), 32)
                pool.sem_inc(s("g2_started"), 1)

            pool.wait_ge(s("y_out"), 32 * NG + 16)

            def item2(n, b, it):
                after(pool, s("vm2"), n, 2)
                gather(b, it, C, table1, idx2, "g2", "i2", "g2_started")
            pairs(pool, item2, NG // 2)
            with pool.If(uncovered(pool) > 0):
                extra_pairs(pool, item2)
                pool.sem_inc(s("g2_started"), 1)

        @block.scalar
        def _(act):
            def a(out_, in_, func, name, **kw):
                return nc.scalar.activation(out_, in_, func, **kw).then_inc(s(name), 1)

            act.wait_ge(s("pad_z"), 1)
            a(iotap, iotaf[:, :], ACT.Copy, "iota_p")
            act.wait_ge(s("pool_c"), 20)
            a(identH[:, :], ident[:, :], ACT.Copy, "iota_p")
            act.wait_ge(s("w_t"), 2)
            a(wT[:, :], pt[0][:, 0:128], ACT.Copy, "w_tc")
            a(weT[:, :], pt[0][:, 128:256], ACT.Copy, "w_tc")
            act.wait_ge(s("w_aux"), 3)
            a(wcat[:, C:TW], pt[1][:, 0:2 * H + 1], ACT.Copy, "w_auxc")
            a(wew[:, :], pt[1][:, 128:256], ACT.Copy, "w_auxc")
            a(bew[:, :], pt[1][:, 256:384], ACT.Copy, "w_auxc")

            def standard_deviation(k):
                act.wait_ge(s("ln_a"), k)
                a(lnw[0:NP, 1, :], lnw[0:NP, 0, :], ACT.Sqrt, "ln_sq", bias=epsc[0:NP, 0:1])

            def normalise(t, b, i):
                return nc.scalar.activation(
                    hb[b][0:NP, i, :], xs[0:NP, bass.DynSlice(t, 1), :].rearrange("p a c -> p (a c)"),
                    ACT.Relu, scale=rstd[0:NP, bass.DynSlice(t, 1)], bias=nmr[0:NP, bass.DynSlice(t, 1)])

            standard_deviation(1)
            act.wait_ge(s("ln_b"), 1)

            def node0(q, b, it):
                after(act, s("h_tr"), q, 2)
                for i in range(2):
                    ins = normalise(q * 2 + i, b, i)
                ins.then_inc(s("h_ready"), 1)
            pairs(act, node0, NQ // 2)
            node0(NQ - 1, 0, NQ // 2)

            def normalise_window(m):
                after(act, s("nmr_f"), m)
                a(fh[:, :], fx[:, :], ACT.Relu, "h_f", scale=fy0[:, 0:1], bias=fnm[:, 0:1])

            def evacuate_window(m):
                after(act, s("ftr_f"), m)
                a(fhT[:, :], finT, ACT.Copy, "ht_f")

            def item(n, b, it, is_extra=False):
                finish_before = not is_extra and not (isinstance(n, int) and n == 0)
                after(act, s("sel_b"), n)
                after(act, s("mg_b"), n, 1)
                a(selH[:, :, :], SEL[b], ACT.Copy, "selh_b")
                after(act, s("thruT_b"), n)
                if not (isinstance(n, int) and n == 0):
                    act.wait_ge(s("tails_b"), n)
                a(thruT[:, :], thruP, ACT.Copy, "thru_c")
                after(act, s("look"), n, 1)
                for r in range(2):
                    act.wait_ge(s("sttr"), n * 2 + (r + 1))
                    a(selT[:, r * 1024:(r + 1) * 1024], ptH[r], ACT.Copy, "stcp")
                after(act, s("fd_b"), n)
                a(fold[b][:, :], fd[:, :], ACT.Exp, "fold_b")
                if finish_before:
                    normalise_window(n - 1)
                after(act, s("zm_b"), n)
                a(wps, lre[:, :, :], ACT.Exp, "wp_b")
                a(V[b][:, :, C:C + H], lre[:, :, :], ACT.Exp, "w_b")
                if finish_before:
                    evacuate_window(n - 1)
            pairs(act, item, NG // 2)
            normalise_window(NG - 1)
            evacuate_window(NG - 1)

            def node1(t, b, it):
                n = t + NQ
                act.wait_ge(s("h_tr"), n - 1)
                normalise(t, b, 0).then_inc(s("h_ready"), 1)
                a(hb[b][0:NP, 1, :], allsum[0:NP, bass.DynSlice(t, 1), TAB:ST].rearrange("p a c -> p (a c)"),
                  ACT.Copy, "y_ready")

            with act.If(uncovered(act) > 0):
                extra_pairs(act, lambda n, b, it: item(n, b, it, True))
                standard_deviation(2)
                act.wait_ge(s("ln_b"), 2)
                pairs(act, node1, NT // 2)

            def item2(n, b, it):
                after(act, s("zt_f"), n)
                a(fhT[:, 0:C], pt[0][:, 0:WIN], ACT.Relu, "zu_f", bias=b1s[:, 0:1])
            pairs(act, item2, NG // 2)

            def node2(t, b, it):
                after(act, s("zc_t"), t, 2)
                a(hb[b][0:NP, 0, :], zin[0:NP, bass.DynSlice(t, 1), :].rearrange("p a c -> p (a c)"),
                  ACT.Copy, "zc_r")
                after(act, s("zc_t"), t)
                a(hT[b][:, 0, 0:NP], pt[b][:, 0:NP], ACT.Relu, "zc_u", bias=b1s[:, 0:1])

            with act.If(uncovered(act) > 0):
                act.wait_ge(s("z_in"), 32)
                pairs(act, node2, NT // 2)

        @block.tensor
        def _(pe):
            pe.wait_ge(s("pool_c"), 20)
            pe.wait_ge(s("consts_in"), 16 * CONSTS)
            nc.tensor.transpose(pt[0][:, 0:128], wcat[:, 0:C], ident[:, :]).then_inc(s("w_t"), 1)
            nc.tensor.transpose(pt[0][:, 128:256], wes[:, :], ident[:, :]).then_inc(s("w_t"), 1)
            pe.wait_ge(s("w_tc"), 2)
            nc.tensor.matmul(pt[1][:, 0:2 * H + 1], wT[:, :], attm[:, :], start=True, stop=True)\
                .then_inc(s("w_aux"), 1)
            nc.tensor.matmul(pt[1][:, 128:256], weT[:, :], w1b[:, :], start=True, stop=True)\
                .then_inc(s("w_aux"), 1)
            pe.wait_ge(s("beb_done"), 1)
            nc.tensor.matmul(pt[1][:, 256:384], beb[:, :], w1b[:, :], start=True, stop=True)\
                .then_inc(s("w_aux"), 1)
            pe.wait_ge(s("w_auxc"), 3)

            def project0(q, b):
                after(pe, s("h_trc"), q)
                for i in range(2):
                    ins = nc.tensor.matmul(pv[b][0:NP, i * TW:(i + 1) * TW], hT[b][:, i, 0:NP], wcat[:, :],
                                           start=True, stop=True)
                ins.then_inc(s("h_mm"), 1)

            def node0(q, b, it):
                after(pe, s("h_ready"), q)
                after(pe, s("h_trc"), q, 2)
                for i in range(2):
                    ins = nc.tensor.transpose(pt[b][:, i * 128:i * 128 + NP], hb[b][0:NP, i, :],
                                              ident[0:NP, 0:NP])
                ins.then_inc(s("h_tr"), 1)
                if not (isinstance(q, int) and q == 0):
                    project0(q - 1, 1 - b)
            pairs(pe, node0, NQ // 2)
            node0(NQ - 1, 0, NQ // 2)
            project0(NQ - 1, 0)

            pe.wait_ge(s("d_f"), 2)
            nc.tensor.matmul(pa[0][:, 0:NG], shp[:, :], dd[:, :, J - 1], start=True, stop=True)\
                .then_inc(s("shifted"), 1)
            nc.tensor.matmul(pa[0][:, 128:128 + NG], shn[:, :], dd[:, :, 0], start=True, stop=True)\
                .then_inc(s("shifted"), 1)
            nc.tensor.matmul(pa[0][:, 256:256 + NG - 1], pick[0][:, :], dd[:, 0:NG - 1, 0], start=True, stop=True)\
                .then_inc(s("shifted"), 1)
            nc.tensor.matmul(pa[0][:, 256 + NG - 1:256 + NG], pick[2][:, :], dd[:, NG - 1, 0:1],
                             start=True, stop=True).then_inc(s("shifted"), 1)
            nc.tensor.matmul(pa[0][:, 384:384 + NG], pick[1][:, :], dd[:, :, J - 1], start=True, stop=True)\
                .then_inc(s("shifted"), 1)

            pe.wait_ge(s("ext_cols"), 1)
            for i in range(3):
                nc.tensor.matmul(pa[1][0:1, i * 128:(i + 1) * 128], extc[:, i:i + 1], ident[:, :],
                                 start=True, stop=True).then_inc(s("ext_mm"), 1)
            nc.tensor.matmul(pa[1][:, 384:512], ones[:, :], extd[:, :], start=True, stop=True)\
                .then_inc(s("ext_mm"), 1)


            def transpose_window(m):
                after(pe, s("h_f"), m)
                after(pe, s("y_f"), m, 1)
                after(pe, s("merged"), m)
                nc.tensor.transpose(finT[:, 0:C], fh[:, :], ident[:, :])
                nc.tensor.transpose(finT[:, C:2 * C], state[:, TAB:ST], ident[:, :]).then_inc(s("ftr_f"), 1)

            def project_window(m):
                after(pe, s("ht_f"), m)
                nc.tensor.matmul(finY, fhT[:, 0:C], w1a[:, :], start=True, stop=False)
                nc.tensor.matmul(finY, fhT[:, C:2 * C], wew[:, :], start=False, stop=True).then_inc(s("ym_f"), 1)

            def item(n, b, it, is_extra=False):
                finish_before = not is_extra and not (isinstance(n, int) and n == 0)
                def attribute_sums(lo, hi):
                    for j in range(lo, hi):
                        ins = nc.tensor.matmul(sumA[b], SEL[b][:, j, :], AT[b][:, j, :],
                                               start=(j == 0), stop=(j == J - 1))
                    return ins

                after(pe, s("thru4_b"), n)
                nc.tensor.transpose(thruP, thru4[b][:, :], ident[:, :]).then_inc(s("thruT_b"), 1)
                after(pe, s("selh_b"), n)
                for r in range(2):
                    if not (isinstance(n, int) and n == 0):
                        pe.wait_ge(s("stcp"), n * 2 + (r - 1))
                    for q in range(8):
                        ins = nc.tensor.transpose(ptH[r][:, q * 128:(q + 1) * 128],
                                                  selH[:, 8 * r + q, :], identH[:, :])
                    ins.then_inc(s("sttr"), 1)
                after(pe, s("pre1_b"), n)
                after(pe, s("thru_c"), n)
                nc.tensor.transpose(tailT, pre1[:, :, J - 1], ident[:, :]).then_inc(s("tailT_b"), 1)
                after(pe, s("tails_b"), n)
                nc.tensor.matmul(cback, tails[:, 0:128], ident[0:H, 0:H], start=True, stop=True)\
                    .then_inc(s("cback_b"), 1)
                pe.wait_ge(s(f"attr{b}"), it * 16 + 16)
                after(pe, s("merged"), n, 2)
                attribute_sums(0, J // 2)
                after(pe, s("pkl_b"), n)
                after(pe, s("pk2_b"), n)
                for j in range(J):
                    ins = nc.tensor.matmul(mg, selH[:, j, :], peaks[:, j, :], start=(j == 0), stop=(j == J - 1))
                ins.then_inc(s("mg_b"), 1)
                attribute_sums(J // 2, J).then_inc(s("am_b"), 1)
                after(pe, s("sh2_b"), n)
                pe.wait_ge(s("stcp"), n * 2 + 2)
                for j in range(J):
                    ins = nc.tensor.matmul(lk[:, j, :], selT[:, j * 128:(j + 1) * 128], parts[b],
                                           start=True, stop=True)
                ins.then_inc(s("look"), 1)
                if finish_before:
                    transpose_window(n - 1)
                after(pe, s("w_b"), n)
                for q in range(4):
                    if q == 2 and finish_before:
                        project_window(n - 1)
                    pe.wait_ge(s("vw_b"), n * 4 + (q + 1))
                    for j in range(q * QUART, (q + 1) * QUART):
                        ins = nc.tensor.matmul(sumV[b], SEL[b][:, j, :], V[b][:, j, :],
                                               start=(j == 0), stop=(j == J - 1))
                    ins.then_inc(s("vm_b"), 1)
            pairs(pe, item, NG // 2)
            transpose_window(NG - 1)
            project_window(NG - 1)

            def project1(t, b):
                pe.wait_ge(s("h_trc"), t + (NQ + 1))
                nc.tensor.matmul(pv[b][0:NP, 0:C], hT[b][:, 0, 0:NP], w1a[:, :], start=True, stop=False)
                nc.tensor.matmul(pv[b][0:NP, 0:C], hT[b][:, 1, 0:NP], wew[:, :], start=False, stop=True)\
                    .then_inc(s("h_mm"), 1)

            def node1(t, b, it):
                after(pe, s("y_ready"), t)
                n = t + NQ
                pe.wait_ge(s("h_ready"), n + 1)
                pe.wait_ge(s("h_trc"), n - 1)
                nc.tensor.transpose(pt[b][:, 0:NP], hb[b][0:NP, 0, :], ident[0:NP, 0:NP])
                nc.tensor.transpose(pt[b][:, 128:128 + NP], hb[b][0:NP, 1, :], ident[0:NP, 0:NP])\
                    .then_inc(s("h_tr"), 1)
                if not (isinstance(t, int) and t == 0):
                    project1(t - 1, 1 - b)
            with pe.If(uncovered(pe) > 0):
                extra_pairs(pe, lambda n, b, it: item(n, b, it, True))
                pairs(pe, node1, NT // 2)
                project1(NT - 1, 1)

            def item2(n, b, it, is_extra=False):
                after(pe, s("sel2"), n)
                pe.wait_ge(s(f"g2{b}"), it * 16 * J + 16 * J)
                after(pe, s("z_add"), n, 2)
                for j in range(J):
                    ins = nc.tensor.matmul(pv[b][:, 0:C], SEL[b][:, j, :], V[b][:, j, 0:C],
                                           start=(j == 0), stop=(j == J - 1))
                ins.then_inc(s("vm2"), 1)
                if is_extra:
                    return
                after(pe, s("z_add"), n)
                after(pe, s("zu_f"), n, 1)
                nc.tensor.transpose(pt[0][:, 0:WIN], state[:, 0:C], ident[:, :]).then_inc(s("zt_f"), 1)
                after(pe, s("zu_f"), n)
                after(pe, s("zo_f"), n, 1)
                nc.tensor.matmul(pa[0][:, 0:C], fhT[:, 0:C], w2s[:, :], start=True, stop=True)\
                    .then_inc(s("zy_f"), 1)
            pairs(pe, item2, NG // 2)

            def node2(t, b, it):
                after(pe, s("zc_r"), t)
                after(pe, s("zc_u"), t, 2)
                nc.tensor.transpose(pt[b][:, 0:NP], hb[b][0:NP, 0, :], ident[0:NP, 0:NP]).then_inc(s("zc_t"), 1)
                after(pe, s("zc_u"), t)
                after(pe, s("zc_o"), t, 2)
                nc.tensor.matmul(pv[b][0:NP, 0:C], hT[b][:, 0, 0:NP], w2s[:, :], start=True, stop=True)\
                    .then_inc(s("zc_m"), 1)
            with pe.If(uncovered(pe) > 0):
                extra_pairs(pe, lambda n, b, it: item2(n, b, it, True))
                pairs(pe, node2, NT // 2)

        @block.vector
        def _(dve):
            v = nc.vector
            count = [0]

            def link(ins):
                count[0] += 1
                ins.then_inc(s("chain"), 1)
                dve.wait_ge(s("chain"), count[0])

            def row(t3, t, lo, hi):
                return t3[0:NP, bass.DynSlice(t, 1), lo:hi].rearrange("p a c -> p (a c)")

            def layernorm(k):
                for i, (first, end) in enumerate(X_CHUNKS):
                    if k == 1:
                        dve.wait_ge(s(f"x_in{i}"), 32)
                    for t in range(first, end):
                        v.bn_stats(stat[0:NP, t, :], xs[0:NP, t, :]).then_inc(s("stats"), 1)
                dve.wait_ge(s("stats"), k * NT)
                m_e, q_e = stat[0:NP, :, 1], stat[0:NP, :, 2]
                m_o, q_o = stat[0:NP, :, 4], stat[0:NP, :, 5]
                w0, w1, w2, w3 = (lnw[0:NP, i, :] for i in range(4))
                link(v.tensor_tensor(w2, m_e, m_o, ALU.subtract))
                link(v.tensor_tensor(w2, w2, w2, ALU.mult))
                link(v.tensor_tensor(w3, q_e, q_o, ALU.add))
                link(v.tensor_scalar(w2, w2, 0.25, None, ALU.mult))
                v.scalar_tensor_tensor(out=w0, in0=w3, scalar=1.0 / C, in1=w2, op0=ALU.mult,
                                       op1=ALU.add).then_inc(s("ln_a"), 1)
                dve.wait_ge(s("ln_a"), k)
                link(v.tensor_tensor(w3, m_e, m_o, ALU.add))
                dve.wait_ge(s("ln_sq"), k)
                link(v.reciprocal(rstd[0:NP, :], w1))
                v.scalar_tensor_tensor(out=nmr[0:NP, :], in0=w3, scalar=-0.5, in1=rstd[0:NP, :],
                                       op0=ALU.mult, op1=ALU.mult).then_inc(s("ln_b"), 1)

            layernorm(1)
            dve.wait_ge(s("unit_z"), 3)

            def result0(q, b):
                after(dve, s("h_mm"), q)
                v.tensor_tensor(tab[0:NP, bass.DynSlice(q * 2, 2), :],
                                pv[b][0:NP, 0:2 * TW].rearrange("p (a c) -> p a c", a=2),
                                unit[0:NP, :].rearrange("p (a c) -> p a c", a=1).to_broadcast([NP, 2, TW]),
                                ALU.add).then_inc(s("h_ev"), 1)

            def transposed(b):
                return pt[b][:, 0:256].rearrange("p (a c) -> p a c", a=2)[:, :, 0:NP]

            def node0(q, b, it):
                after(dve, s("h_tr"), q)
                v.tensor_copy(hT[b][:, :, 0:NP], transposed(b)).then_inc(s("h_trc"), 1)
                if not (isinstance(q, int) and q == 0):
                    result0(q - 1, 1 - b)
            pairs(dve, node0, NQ // 2)
            node0(NQ - 1, 0, NQ // 2)
            result0(NQ - 1, 0)
            dve.wait_ge(s("h_ev"), NQ)
            dl = tab[0:NP, :, TAB:TW]
            dp = [dlog[0:NP, :, H:DL].bitcast(BF16)[:, :, k * H:(k + 1) * H] for k in range(NK)]
            v.tensor_copy(dlog[0:NP, :, 0:H], dl).then_inc(s("dl"), 1)
            v.tensor_copy(dp[0], dl).then_inc(s("dl"), 1)
            dve.wait_ge(s("dl"), 2)
            v.tensor_tensor(dres[0:NP, :, :], dl, dp[0], ALU.subtract).then_inc(s("dl"), 1)
            dve.wait_ge(s("dl"), 3)
            v.tensor_copy(dp[1], dres[0:NP, :, :]).then_inc(s("dl"), 1)
            dve.wait_ge(s("dl"), 4)
            v.tensor_tensor(dp[2], dres[0:NP, :, :], dp[1], ALU.subtract).then_inc(s("dl_done"), 1)

            dve.wait_ge(s("d_f"), 2)
            dve.wait_ge(s("shifted"), 5)
            dve.wait_ge(s("pool_c"), 20)
            prev, nxt = pa[0][:, 0:NG], pa[0][:, 128:128 + NG]
            v.tensor_scalar(basei[0:1, :], pa[0][0:1, 256:256 + NG], float(TOP), None, ALU.min)\
                .then_inc(s("base_i"), 1)
            v.tensor_scalar(firsts[:, :], pa[0][:, 256:256 + NG], float(TOP), None, ALU.min)\
                .then_inc(s("masks"), 1)
            v.tensor_copy(lasts[:, :], pa[0][:, 384:384 + NG]).then_inc(s("masks"), 1)
            v.scalar_tensor_tensor(out=isl[:, :, J - 1], in0=nxt, scalar=edgefix[:, 1:2], in1=dd[:, :, J - 1],
                                   op0=ALU.add, op1=ALU.not_equal).then_inc(s("masks"), 1)
            v.scalar_tensor_tensor(out=cin[:, :], in0=prev, scalar=edgefix[:, 0:1], in1=dd[:, :, 0],
                                   op0=ALU.add, op1=ALU.not_equal).then_inc(s("masks"), 1)
            v.scalar_tensor_tensor(out=thru[:, :], in0=prev, scalar=edgefix[:, 0:1], in1=dd[:, :, J - 1],
                                   op0=ALU.add, op1=ALU.not_equal).then_inc(s("masks"), 1)
            dve.wait_ge(s("masks"), 5)
            for m in (cin[:, :], thru[:, :]):
                v.tensor_scalar(m, m, -BIG, None, ALU.mult).then_inc(s("masks"), 1)
            v.tensor_tensor(drel[:, :, :], dd[:, :, :], firsts[:, :].rearrange("p (g a) -> p g a", a=1)
                            .to_broadcast([128, NG, J]), ALU.subtract).then_inc(s("masks"), 1)
            dve.wait_ge(s("masks"), 8)
            dve.wait_ge(s("pmasks"), 4)

            def estep(ins):
                ins.then_inc(s("ext"), 1)
                ext_count[0] += 1
                dve.wait_ge(s("ext"), ext_count[0])
            ext_count = [0]
            dve.wait_ge(s("rank_b"), 3)
            shift_by = WIN.bit_length() - 1
            assert 1 << shift_by == WIN
            estep(v.tensor_tensor(spani[:, :], lasts[:, :], firsts[:, :], ALU.subtract))
            estep(v.tensor_scalar(spani[:, :], spani[:, :], shift_by, None, ALU.arith_shift_right))
            estep(v.tensor_copy(wins[:, :], spani[:, :]))
            estep(v.tensor_tensor_scan(upto[:, :], onef[:, :], wins[:, :], 0.0, ALU.mult, ALU.add))
            estep(v.tensor_scalar(before[:, :], upto[:, :], rank[:, 0:1], None, ALU.is_le))
            estep(v.tensor_reduce(extc[:, 0:1], before[:, :], AX.X, ALU.add))
            estep(v.tensor_tensor(extw[:, :], before[:, :], wins[:, :], ALU.mult))
            estep(v.tensor_reduce(extc[:, 3:4], extw[:, :], AX.X, ALU.add))
            estep(v.tensor_scalar(extw[:, :], iotaf[:, 0:NG], extc[:, 0:1], None, ALU.is_equal))
            estep(v.tensor_tensor(extw[:, :], extw[:, :], firsts[:, :], ALU.mult))
            estep(v.tensor_reduce(extc[:, 4:5], extw[:, :], AX.X, ALU.add))
            estep(v.tensor_tensor(extc[:, 3:4], rank[:, :], extc[:, 3:4], ALU.subtract))
            estep(v.tensor_scalar(extc[:, 3:4], extc[:, 3:4], 1.0, float(WIN), ALU.add, ALU.mult))
            estep(v.tensor_tensor(extc[:, 1:2], extc[:, 4:5], extc[:, 3:4], ALU.add))
            estep(v.tensor_scalar(extc[:, 5:6], extc[:, 0:1], NG - 0.5, None, ALU.is_lt))
            estep(v.tensor_tensor(extc[:, 0:1], extc[:, 0:1], extc[:, 5:6], ALU.mult))
            estep(v.tensor_scalar(extc[:, 1:2], extc[:, 1:2], float(DUMMY), extc[:, 5:6], ALU.subtract, ALU.mult))
            estep(v.tensor_scalar(extc[:, 1:2], extc[:, 1:2], float(DUMMY), None, ALU.add))
            estep(v.tensor_scalar(extc[:, 2:3], extc[:, 0:1], float(GE), float(LAST), ALU.mult, ALU.min))
            v.tensor_scalar(extd[:, :], ident[:, :], extc[:, 1:2], None, ALU.mult).then_inc(s("ext_cols"), 1)
            dve.wait_ge(s("ext_mm"), 4)
            for i in range(3):
                v.tensor_copy(extrow[i][0:1, :], pa[1][0:1, i * 128:(i + 1) * 128]).then_inc(s("ext_done"), 1)
            v.tensor_copy(extb[:, :], pa[1][:, 384:512]).then_inc(s("ext_done"), 1)
            estep(v.tensor_tensor(extw[0:1, 0:NG - 1], firsts[0:1, 1:NG], firsts[0:1, 0:NG - 1], ALU.subtract))
            estep(v.tensor_reduce(flag[0:1, 0:1], extw[0:1, 0:NG - 1], AX.X, ALU.max))
            estep(v.tensor_scalar(flag[0:1, 0:1], flag[0:1, 0:1], float(-WIN), None, ALU.add))
            estep(v.tensor_copy(flag[0:1, 1:2], firsts[0:1, 0:1]))
            estep(v.tensor_scalar(flag[0:1, 2:3], firsts[0:1, NG - 1:NG], -1.0, float(TOP), ALU.mult, ALU.add))
            estep(v.tensor_copy(flag[0:1, 3:4], upto[0:1, NG - 1:NG]))
            estep(v.tensor_reduce(flag[0:1, 4:5], flag[0:1, 0:4], AX.X, ALU.max))
            v.tensor_scalar(extn[0:1, 0:1], flag[0:1, 4:5], 0.0, None, ALU.max).then_inc(s("ext_done"), 1)

            dve.wait_ge(s("iota_p"), 1)

            def select(n, b, name, extra_group=None, fetched=None):
                if extra_group is None:
                    at = drel[:, bass.DynSlice(n, 1), :].rearrange("p a (j c) -> p (a j) c", c=1)
                else:
                    v.tensor_scalar(drx[b][:, :], dd[:, bass.DynSlice(extra_group, 1), :]
                                    .rearrange("p a j -> p (a j)"), extb[:, bass.DynSlice(n - NG, 1)], None,
                                    ALU.subtract).then_inc(s(fetched), 1)
                    dve.wait_ge(s(fetched), n - (NG - 1))
                    at = drx[b][:, :].rearrange("p (j c) -> p j c", c=1)
                v.tensor_tensor(SEL[b], iotap.rearrange("p (a w) -> p a w", a=1).to_broadcast([128, J, WIN]),
                                at.to_broadcast([128, J, WIN]), ALU.is_equal).then_inc(s(name), 1)

            def split(n, k, full, rest, part, sems):
                known, s_rest, *s_part = sems
                if k == 0:
                    after(dve, s(known), n)
                    v.tensor_copy(part[0], full).then_inc(s(s_part[0]), 1)
                elif k == 1:
                    after(dve, s(s_part[0]), n)
                    v.tensor_tensor(rest, full, part[0], ALU.subtract).then_inc(s(s_rest), 1)
                elif k == 2:
                    after(dve, s(s_rest), n)
                    v.tensor_copy(part[1], rest).then_inc(s(s_part[1]), 1)
                else:
                    after(dve, s(s_part[1]), n)
                    v.tensor_tensor(part[2], rest, part[1], ALU.subtract).then_inc(s(s_part[2]), 1)

            def split_peaks(n, k):
                split(n, k, pkf[:, :, :], pkr[:, :, :], [peaks[:, :, i * H:(i + 1) * H] for i in range(NK)],
                      ("pkf_b", "pr_b", "pk_b", "pk1_b", "pk2_b"))

            def split_shift(n, b, k):
                split(n, k, node[b][:, SH:SH + H], shr[:, :],
                      [parts[b][:, (NK + i) * H:(NK + i + 1) * H] for i in range(NK)],
                      ("node_b", "sr_b", "sh0_b", "sh1_b", "sh2_b"))

            def rescale_state(n, b):
                dve.wait_ge(s("s_load"), n * 16 + 16)
                after(dve, s("fold_b"), n)
                st4 = state[:, 0:C].rearrange("p (h f) -> p h f", f=F)
                v.tensor_tensor(st4, st4, fold[b][:, :].rearrange("p (h a) -> p h a", a=1)
                                .to_broadcast([128, H, F]), ALU.mult).then_inc(s("ms_b"), 1)
                v.tensor_tensor(state[:, C:C + H], state[:, C:C + H], fold[b][:, :], ALU.mult)\
                    .then_inc(s("mt_b"), 1)

            def add_sums(n, b):
                dve.wait_ge(s("vm_b"), n * 4 + 4)
                after(dve, s("ms_b"), n)
                after(dve, s("mt_b"), n)
                after(dve, s("am_b"), n)
                v.tensor_tensor(state[:, :], state[:, :], sums[b], ALU.add).then_inc(s("merged"), 1)

            def done(m, k):
                dve.wait_ge(s("fin"), m * FIN + k)

            def finish_weights(m):
                after(dve, s("merged"), m)
                v.reciprocal(frd[:, :], state[:, C:C + H]).then_inc(s("fin"), 1)
                after(dve, s("y_f"), m, 1)
                v.tensor_copy(fdeg[:, :], state[:, TAB - 1:TAB]).then_inc(s("fin"), 1)

            def finish_mean(m):
                done(m, 2)
                v.tensor_tensor(fo[:, :].rearrange("p (h f) -> p h f", f=F),
                                state[:, 0:C].rearrange("p (h f) -> p h f", f=F),
                                frd[:, :].rearrange("p (h a) -> p h a", a=1).to_broadcast([128, H, F]), ALU.mult)\
                    .then_inc(s("fin"), 1)

            def finish_bias(m):
                done(m, 3)
                v.tensor_tensor(fo[:, :], fo[:, :], b0s[:, :], ALU.add).then_inc(s("fin"), 1)

            def finish_residual(m):
                done(m, 4)
                dve.wait_ge(s("xw_load"), m * 16 + 16)
                v.scalar_tensor_tensor(out=fx[:, :], in0=fo[:, :], scalar=0.0, in1=fxw[:, :],
                                       op0=ALU.max, op1=ALU.add).then_inc(s("x1_f"), 1)

            def finish_stats(m):
                after(dve, s("x1_f"), m)
                v.bn_stats(fst[:, :], fx[:, :]).then_inc(s("fin"), 1)

            def finish_b2(m):
                after_dma(dve, s("xb_out"), m)
                v.tensor_tensor(fxb[:, :], fx[:, :], b2s[:, :], ALU.add).then_inc(s("xb_f"), 1)

            def finish_variance(m):
                done(m, 5)
                dve.sem_inc(s("fin_turn"), 1)
                v.bn_aggr(fmv[:, :], fst[:, :]).then_inc(s("fin"), 1)

            def finish_eps(m):
                done(m, 6)
                v.tensor_scalar(fve[:, :], fmv[:, 1:2], EPS, None, ALU.add).then_inc(s("fin"), 1)

            def finish_halve(m):
                done(m, 7)
                v.tensor_scalar(fy1[:, :].bitcast(INT32), fve[:, :].bitcast(INT32), 1, None,
                                ALU.arith_shift_right).then_inc(s("fin"), 1)

            def finish_guess(m):
                done(m, 8)
                v.tensor_scalar(fy0[:, :].bitcast(INT32), fy1[:, :].bitcast(INT32), -1.0, float(MAGIC),
                                ALU.mult, ALU.add).then_inc(s("fin"), 1)

            def newton_square(m, r):
                done(m, 9 + 3 * r)
                v.scalar_tensor_tensor(out=fy1[:, :], in0=fy0[:, :], scalar=fve[:, 0:1], in1=fy0[:, :],
                                       op0=ALU.mult, op1=ALU.mult).then_inc(s("fin"), 1)

            def newton_factor(m, r):
                done(m, 10 + 3 * r)
                v.tensor_scalar(fy1[:, :], fy1[:, :], -0.5, 1.5, ALU.mult, ALU.add).then_inc(s("fin"), 1)

            def newton_step(m, r):
                done(m, 11 + 3 * r)
                v.tensor_tensor(fy0[:, :], fy0[:, :], fy1[:, :], ALU.mult).then_inc(s("fin"), 1)

            def finish_shift(m):
                done(m, 18)
                v.scalar_tensor_tensor(out=fnm[:, :], in0=fmv[:, 0:1], scalar=-1.0, in1=fy0[:, :],
                                       op0=ALU.mult, op1=ALU.mult).then_inc(s("nmr_f"), 1)

            def finish_projection(m):
                after(dve, s("ym_f"), m)
                dve.wait_ge(s("y_out"), m * 32 + 16)
                v.scalar_tensor_tensor(out=fy[:, :], in0=bew[:, :], scalar=fdeg[:, 0:1], in1=finY,
                                       op0=ALU.mult, op1=ALU.add).then_inc(s("y_f"), 1)

            def item(n, b, it, g=None):
                is_extra = g is not None
                first = is_extra or (isinstance(n, int) and n == 0)
                m = None if first else n - 1

                def between(step, *more):
                    if m is not None:
                        step(m, *more)

                if not (isinstance(n, int) and n < 2):
                    dve.wait_ge(s("vm_b"), n * 4 - 4)
                select(n, b, "sel_b", g, "drx_b")
                g = g if is_extra else n
                after(dve, s("thruT_b"), n, 1)
                v.tensor_copy(thru4[b][:, :], thru[:, bass.DynSlice(g, 1)].to_broadcast([128, H]))\
                    .then_inc(s("thru4_b"), 1)
                v.tensor_copy(cont4[:, :, :], cont[:, bass.DynSlice(g, 1), :].to_broadcast([128, H, J]))\
                    .then_inc(s("cont_b"), 1)
                if m is not None:
                    rescale_state(m, 1 - b)
                dve.wait_ge(s(f"gat{b}"), it * 16 * J + 16 * J)
                v.tensor_copy(logit[:, :, :], V[b][:, :, C:C + H].rearrange("p j h -> p h j"))\
                    .then_inc(s("log_b"), 1)
                after(dve, s("cont_b"), n)
                after(dve, s("log_b"), n)
                flat = "p h j -> p (h j)"
                v.tensor_tensor_scan(pre1[:, :, :].rearrange(flat), cont4[:, :, :].rearrange(flat),
                                     logit[:, :, :].rearrange(flat), -BIG, ALU.add, ALU.max)\
                    .then_inc(s("pre1_b"), 1)
                if m is not None:
                    add_sums(m, 1 - b)
                if not (is_extra or (isinstance(n, int) and n < 2)):
                    finish_projection(n - 2)
                after(dve, s("thru_c"), n)
                after(dve, s("tailT_b"), n)
                v.tensor_tensor_scan(tails[:, 1:129], thruT[:, :], tailT, -BIG, ALU.add, ALU.max)\
                    .then_inc(s("tails_b"), 1)
                between(finish_weights)
                between(finish_mean)
                after(dve, s("cback_b"), n)
                v.scalar_tensor_tensor(out=logit[:, :, 0], in0=cback, scalar=cin[:, bass.DynSlice(g, 1)],
                                       in1=logit[:, :, 0], op0=ALU.add, op1=ALU.max).then_inc(s("carry_b"), 1)
                between(finish_bias)
                after(dve, s("carry_b"), n)
                v.tensor_tensor_scan(pre2[:, :, :].rearrange(flat), cont4[:, :, :].rearrange(flat),
                                     logit[:, :, :].rearrange(flat), -BIG, ALU.add, ALU.max)\
                    .then_inc(s("pre2_b"), 1)
                between(finish_residual)
                last = isl[:, bass.DynSlice(g, 1), :].rearrange("p a (j c) -> p (a j) c", c=1)
                v.tensor_copy(peaks[:, :, NK * H:NK * H + 1], last).then_inc(s("pkl_b"), 1)
                after(dve, s("pre2_b"), n)
                v.tensor_tensor(pkf[:, :, :], pre2[:, :, :].rearrange("p h j -> p j h"),
                                last.to_broadcast([128, J, H]), ALU.mult).then_inc(s("pkf_b"), 1)
                between(finish_stats)
                split_peaks(n, 0)
                between(finish_variance)
                split_peaks(n, 1)
                between(finish_eps)
                split_peaks(n, 2)
                between(finish_halve)
                split_peaks(n, 3)
                between(finish_guess)
                between(finish_b2)
                between(newton_square, 0)
                after(dve, s("mg_b"), n)
                v.tensor_scalar(pen[:, :], mg[:, NK * H:NK * H + 1], -1.0, BIG, ALU.add, ALU.mult)\
                    .then_inc(s("pen_b"), 1)
                v.tensor_reduce(mgs[:, :], mg[:, 0:NK * H].rearrange("p (k h) -> p h k", h=H),
                                AX.X, ALU.add).then_inc(s("mgs_b"), 1)
                between(newton_factor, 0)
                dve.wait_ge(s("st_load"), n * 32 + 32)
                after(dve, s("pen_b"), n)
                after(dve, s("mgs_b"), n)
                v.scalar_tensor_tensor(out=newold[b][:, 0, :], in0=mgs[:, :], scalar=pen[:, 0:1],
                                       in1=newold[b][:, 1, :], op0=ALU.add, op1=ALU.max)\
                    .then_inc(s("mnew_b"), 1)
                between(newton_step, 0)
                after(dve, s("mnew_b"), n)
                v.tensor_tensor(nu[:, :].rearrange("p (a h) -> p a h", h=H), newold[b][:, :, :],
                                node[b][:, 0:H].rearrange("p (a h) -> p a h", a=1).to_broadcast([128, 2, H]),
                                ALU.add).then_inc(s("nu_b"), 1)
                between(newton_square, 1)
                after(dve, s("nu_b"), n)
                v.scalar_tensor_tensor(out=node[b][:, SH:SH + 2 * H], in0=nu[:, :], scalar=SLOPE, in1=nu[:, :],
                                       op0=ALU.mult, op1=ALU.max).then_inc(s("node_b"), 1)
                between(newton_factor, 1)
                split_shift(n, b, 0)
                between(newton_step, 1)
                split_shift(n, b, 1)
                between(newton_square, 2)
                split_shift(n, b, 2)
                between(newton_factor, 2)
                split_shift(n, b, 3)
                v.tensor_tensor(fd[:, :], node[b][:, SH + H:SH + 2 * H], node[b][:, SH:SH + H], ALU.subtract)\
                    .then_inc(s("fd_b"), 1)
                between(newton_step, 2)
                between(finish_shift)
                after(dve, s("look"), n)
                v.tensor_reduce(lks[:, :, :].rearrange("p j (g h) -> p (j g) h", h=H),
                                lk.rearrange("p j (g k h) -> p (j g) h k", k=NK, h=H), AX.X, ALU.add)\
                    .then_inc(s("lks_b"), 1)
                after(dve, s("lks_b"), n)
                v.tensor_tensor(lin[:, :, :], V[b][:, :, C:C + H], lks[:, :, 0:H], ALU.add).then_inc(s("lin_b"), 1)
                after(dve, s("lin_b"), n)
                v.scalar_tensor_tensor(out=lre[:, :, :], in0=lin[:, :, :], scalar=SLOPE, in1=lin[:, :, :],
                                       op0=ALU.mult, op1=ALU.max).then_inc(s("lre_b"), 1)
                after(dve, s("lre_b"), n)
                v.tensor_tensor(lin[:, :, :], lre[:, :, :], lks[:, :, H:2 * H], ALU.subtract)\
                    .then_inc(s("zs_b"), 1)
                after(dve, s("zs_b"), n)
                v.tensor_scalar(lre[:, :, :], lin[:, :, :], 0.0, None, ALU.min).then_inc(s("zm_b"), 1)
                after(dve, s("wp_b"), n)
                for q in range(4):
                    js = slice(q * QUART, (q + 1) * QUART)
                    v4 = V[b][:, js, 0:C].rearrange("p j (h f) -> p j h f", f=F)
                    v.tensor_tensor(v4, v4, wps[:, js, :].rearrange("p j (h a) -> p j h a", a=1)
                                    .to_broadcast([128, QUART, H, F]), ALU.mult).then_inc(s("vw_b"), 1)
                if is_extra:
                    rescale_state(n, b)
                    add_sums(n, b)
            pairs(dve, item, NG // 2)
            m = NG - 1
            rescale_state(m, 1)
            add_sums(m, 1)
            finish_projection(m - 1)
            for step in (finish_weights, finish_mean, finish_bias, finish_residual, finish_stats, finish_variance,
                         finish_b2, finish_eps, finish_halve, finish_guess):
                step(m)
            for r in range(3):
                newton_square(m, r)
                newton_factor(m, r)
                newton_step(m, r)
            finish_shift(m)
            finish_projection(m)

            with dve.If(uncovered(dve) > 0):
                extra_pairs(dve, lambda n, b, it: item(n, b, it, extra(dve, 0, n, NG - 1)))
                dve.wait_ge(s("sum_in"), 32)
                dn = allsum[0:NP, :, C:C + H]
                link(v.reciprocal(rden[0:NP, :, :], dn))
                for h in range(H):
                    part = allsum[0:NP, :, h * F:(h + 1) * F]
                    link(v.tensor_tensor(part, part, rden[0:NP, :, h:h + 1].to_broadcast([NP, NT, F]), ALU.mult))
                full = allsum[0:NP, :, 0:C]
                link(v.tensor_tensor(full, full, b0s[0:NP, :].rearrange("p (a c) -> p a c", a=1)
                                     .to_broadcast([NP, NT, C]), ALU.add))
                link(v.scalar_tensor_tensor(out=xs[0:NP, :, :], in0=full, scalar=0.0, in1=xs[0:NP, :, :],
                                            op0=ALU.max, op1=ALU.add))
                layernorm(2)

                def result1(t, b):
                    dve.wait_ge(s("h_mm"), t + (NQ + 1))
                    v.scalar_tensor_tensor(out=row(tab, t, 0, C), in0=bew[0:NP, :],
                                           scalar=row(allsum, t, TAB - 1, TAB), in1=pv[b][0:NP, 0:C],
                                           op0=ALU.mult, op1=ALU.add).then_inc(s("h_ev"), 1)

                def node1(t, b, it):
                    dve.wait_ge(s("h_tr"), t + (NQ + 1))
                    v.tensor_copy(hT[b][:, :, 0:NP], transposed(b)).then_inc(s("h_trc"), 1)
                    if not (isinstance(t, int) and t == 0):
                        result1(t - 1, 1 - b)
                pairs(dve, node1, NT // 2)
                result1(NT - 1, 1)
                dve.wait_ge(s("h_ev"), NQ + NT)
                v.tensor_copy(pen[:, :], b1s[:, :]).then_inc(s("tab1_done"), 1)
                v.tensor_tensor(xs[0:NP, :, :], xs[0:NP, :, :], b2s[0:NP, :].rearrange("p (a c) -> p a c", a=1)
                                .to_broadcast([NP, NT, C]), ALU.add).then_inc(s("b2add"), 1)

            def item2(n, b, it, g=None):
                after(dve, s("vm2"), n, 2)
                select(n, b, "sel2", g, "drx2_b")
                dve.wait_ge(s("z_load"), n * 16 + 16)
                after(dve, s("vm2"), n)
                v.tensor_tensor(state[:, 0:C], state[:, 0:C], pv[b][:, 0:C], ALU.add).then_inc(s("z_add"), 1)
                if g is not None:
                    return
                dve.wait_ge(s("xr_load"), n * 16 + 16)
                after_dma(dve, s("z_out"), n)
                after(dve, s("zy_f"), n)
                v.tensor_tensor(fy[:, :], pa[0][:, 0:C], fxw[:, :], ALU.add).then_inc(s("zo_f"), 1)
            pairs(dve, item2, NG // 2)

            def node2(t, b, it):
                after(dve, s("zc_m"), t)
                v.tensor_tensor(row(tab, t, 0, C), pv[b][0:NP, 0:C], row(xs, t, 0, C), ALU.add)\
                    .then_inc(s("zc_o"), 1)

            with dve.If(uncovered(dve) > 0):
                extra_pairs(dve, lambda n, b, it: item2(n, b, it, extra(dve, 0, n, NG - 1)))
                dve.wait_ge(s("b2add"), 1)
                pairs(dve, node2, NT // 2)


CONSTS = 1 + 2 * H + 4 + 2 + 2
PADS = 0
for _wd in (DL, H, ST, C):
    PADS += -(-((NPAD - N) // 75 * _wd) // (ST - C - H))

_INS = ['x', 'src', 'dst', 'edge_attr_128', 'L0_gnn_W', 'L0_gnn_att_src', 'L0_gnn_att_dst', 'L0_gnn_bias',
        'L1_gnn_We', 'L1_gnn_be', 'L1_gnn_W1', 'L1_gnn_b1', 'L1_gnn_W2', 'L1_gnn_b2']


def kernel(**inputs):
    import numpy as _np
    import concourse.bacc as _bacc
    from concourse import mybir as _mybir
    from concourse.bass_utils import run_bass_kernel_spmd as _run

    nc = _bacc.Bacc("TRN2", target_bir_lowering=False, num_devices=1)
    arrays, args = {}, []
    for name in _INS:
        a = _np.ascontiguousarray(inputs[name])
        arrays[f"in_{name}_dram"] = a
        args.append(nc.dram_tensor(f"in_{name}_dram", a.shape, _mybir.dt.from_np(a.dtype), kind="ExternalInput").ap())
    args.append(nc.dram_tensor("out_0_dram", (N, C), _mybir.dt.float32, kind="ExternalOutput").ap())
    gnn_kernel(nc, *args)
    r = _run(nc, [arrays], core_ids=[0])
    return r.results[0]["out_0_dram"]
```
